# Optimizing a Trainium2 kernel written in Bass

```python
import numpy as np
import jax
import jax.numpy as jnp

def _softmax(x, axis=-1):
    return jax.nn.softmax(x, axis=axis)
def _gelu(x):
    return jax.nn.gelu(x, approximate=True)
def _silu(x):
    return jax.nn.silu(x)
def _sigmoid(x):
    return jax.nn.sigmoid(x)
def _layernorm(x, axis=-1, eps=1e-5):
    m = jnp.mean(x, axis=axis, keepdims=True)
    v = jnp.var(x, axis=axis, keepdims=True)
    return (x - m) / jnp.sqrt(v + eps)
def _scatter_add(tgt, idx, src, axis=0):
    return tgt.at[idx].add(src)
def _segment_sum(src, seg, n):
    return jax.ops.segment_sum(src, seg, n)

kernel_name = 'mk_conv_seq_d1_conv_nchw256_3f3193'

def setup_inputs(seed: int = 0):
    np.random.seed(seed)
    _w = jnp.asarray
    def _rec_inputs():
        import jax
        import jax.numpy as jnp
        _gk = jax.random.key(seed)
        x = -0.0002023 + 1 * jax.random.normal(jax.random.fold_in(_gk, 1), (32, 256, 28, 28), jnp.float32)
        return x
    x = _rec_inputs()
    def _L0_conv_setup():
        import jax, jax.numpy as jnp
        import numpy as np
        KH = KW = 9
        PAD = KH // 2
        NUM_LEVELS = 2
        ANG_LEVELS = 6
        FACBASE = 2
        NBINS = NUM_LEVELS * ANG_LEVELS
        BH, BW = (4, 3)
        EPS = 1e-05
        DN = ('NCHW', 'OIHW', 'NCHW')

        def _logpolar_masks():
            masks = np.zeros((NBINS, 1, KH, KW), np.float32)
            cy, cx = (KH // 2, KW // 2)
            two_pi = 2.0 * np.pi
            for i in range(KH):
                for j in range(KW):
                    dy, dx = (i - cy, j - cx)
                    r = np.hypot(dy, dx)
                    if r < 1.0:
                        continue
                    lev = int(np.floor(np.log(r) / np.log(FACBASE)))
                    lev = min(max(lev, 0), NUM_LEVELS - 1)
                    th = np.arctan2(dy, dx) % two_pi
                    ang = min(int(th / (two_pi / ANG_LEVELS)), ANG_LEVELS - 1)
                    masks[lev * ANG_LEVELS + ang, 0, i, j] = 1.0
            cnt = masks.sum(axis=(1, 2, 3), keepdims=True)
            return masks / np.maximum(cnt, 1.0)
        _MASKS = _logpolar_masks()

        def log_pooling(x):
            B, C, H, W = x.shape
            k = jnp.asarray(_MASKS, dtype=x.dtype)
            y = jax.lax.conv_general_dilated(x.reshape(B * C, 1, H, W), k, (1, 1), [(PAD, PAD), (PAD, PAD)], dimension_numbers=DN)
            y = y.reshape(B, C, BH, BW, H, W)
            y = y.transpose(0, 1, 4, 2, 5, 3)
            return y.reshape(B, C, BH * H, BW * W)
        key = jax.random.key(seed)
        ks = jax.random.split(key, 4)
        B, C, H, W = (32, 256, 28, 28)
        return {'x': jax.random.normal(ks[0], (B, C, H, W), jnp.float32), 'w_conv1': jax.random.normal(ks[1], (C, C, BH, BW), jnp.float32) * 0.02, 'w_center': jax.random.normal(ks[2], (C, C, 1, 1), jnp.float32) * 0.05, 'b_center': jax.random.normal(ks[3], (C,), jnp.float32) * 0.01, 'gamma': jnp.ones((C,), jnp.float32), 'beta': jnp.zeros((C,), jnp.float32)}
    _L0_conv_all = _L0_conv_setup()
    _L0_conv_in = {k: v for k, v in _L0_conv_all.items() if k in ('w_conv1', 'w_center', 'b_center', 'gamma', 'beta', )}
    del _L0_conv_all

    return {
        "x": x,
        "L0_conv_w_conv1": _L0_conv_in["w_conv1"],
        "L0_conv_w_center": _L0_conv_in["w_center"],
        "L0_conv_b_center": _L0_conv_in["b_center"],
        "L0_conv_gamma": _L0_conv_in["gamma"],
        "L0_conv_beta": _L0_conv_in["beta"],
    }

def reference(x, L0_conv_w_conv1, L0_conv_w_center, L0_conv_b_center, L0_conv_gamma, L0_conv_beta):
    import jax
    import jax.numpy as jnp
    def _L0_conv_ref(x, w_conv1, w_center, b_center, gamma, beta):
        import jax, jax.numpy as jnp
        import numpy as np
        KH = KW = 9
        PAD = KH // 2
        NUM_LEVELS = 2
        ANG_LEVELS = 6
        FACBASE = 2
        NBINS = NUM_LEVELS * ANG_LEVELS
        BH, BW = (4, 3)
        EPS = 1e-05
        DN = ('NCHW', 'OIHW', 'NCHW')

        def _logpolar_masks():
            masks = np.zeros((NBINS, 1, KH, KW), np.float32)
            cy, cx = (KH // 2, KW // 2)
            two_pi = 2.0 * np.pi
            for i in range(KH):
                for j in range(KW):
                    dy, dx = (i - cy, j - cx)
                    r = np.hypot(dy, dx)
                    if r < 1.0:
                        continue
                    lev = int(np.floor(np.log(r) / np.log(FACBASE)))
                    lev = min(max(lev, 0), NUM_LEVELS - 1)
                    th = np.arctan2(dy, dx) % two_pi
                    ang = min(int(th / (two_pi / ANG_LEVELS)), ANG_LEVELS - 1)
                    masks[lev * ANG_LEVELS + ang, 0, i, j] = 1.0
            cnt = masks.sum(axis=(1, 2, 3), keepdims=True)
            return masks / np.maximum(cnt, 1.0)
        _MASKS = _logpolar_masks()

        def log_pooling(x):
            B, C, H, W = x.shape
            k = jnp.asarray(_MASKS, dtype=x.dtype)
            y = jax.lax.conv_general_dilated(x.reshape(B * C, 1, H, W), k, (1, 1), [(PAD, PAD), (PAD, PAD)], dimension_numbers=DN)
            y = y.reshape(B, C, BH, BW, H, W)
            y = y.transpose(0, 1, 4, 2, 5, 3)
            return y.reshape(B, C, BH * H, BW * W)
        xp = log_pooling(x)
        out = jax.lax.conv_general_dilated(xp, w_conv1, (BH, BW), 'VALID', dimension_numbers=DN)
        out = out + jax.lax.conv_general_dilated(x, w_center, (1, 1), 'VALID', dimension_numbers=DN)
        out = out + b_center[None, :, None, None]
        mean = out.mean(axis=(0, 2, 3), keepdims=True)
        var = out.var(axis=(0, 2, 3), keepdims=True)
        out = (out - mean) * jax.lax.rsqrt(var + EPS)
        out = out * gamma[None, :, None, None] + beta[None, :, None, None]
        return jax.nn.relu(out + x)

    def _gn(v, G=32, eps=1e-5):
        B_, C_, H_, W_ = v.shape
        g = v.reshape(B_, G, C_ // G, H_, W_)
        m = jnp.mean(g, axis=(2, 3, 4), keepdims=True)
        s = jnp.var(g, axis=(2, 3, 4), keepdims=True)
        return ((g - m) / jnp.sqrt(s + eps)).reshape(v.shape)

    def _ln_c(v, eps=1e-6):
        m = jnp.mean(v, axis=1, keepdims=True)
        s = jnp.var(v, axis=1, keepdims=True)
        return (v - m) / jnp.sqrt(s + eps)

    def _ln_t(v, eps=1e-5):
        m = jnp.mean(v, axis=-1, keepdims=True)
        s = jnp.var(v, axis=-1, keepdims=True)
        return (v - m) / jnp.sqrt(s + eps)

    def _to_tokens(v):
        B_, C_, H_, W_ = v.shape
        return v.reshape(B_, C_, H_ * W_).transpose(0, 2, 1)
    def _from_tokens(t, like):
        B_, C_, H_, W_ = like.shape
        return t.transpose(0, 2, 1).reshape(B_, C_, H_, W_)

    x = _L0_conv_ref(x, L0_conv_w_conv1, L0_conv_w_center, L0_conv_b_center, L0_conv_gamma, L0_conv_beta)
    return x


_drawn_inputs = setup_inputs


def setup_inputs(seed=0):
    import zlib

    import numpy as np

    out = dict(_drawn_inputs(seed))
    spreads = {'L0_conv_gamma': (1.0, 0.2), 'L0_conv_beta': (0.0, 0.1)}
    factors = {}
    for name, (base, spread) in spreads.items():
        noise = np.random.default_rng([zlib.crc32(name.encode()), seed]).standard_normal(out[name].shape)
        drawn = base * np.exp(spread * noise) if base else spread * noise
        out[name] = jnp.asarray(drawn.astype(out[name].dtype))
    for name, factor in factors.items():
        out[name] = (out[name] * factor).astype(out[name].dtype)
    return out
```

```python
from contextlib import ExitStack

import concourse.bass as bass
from concourse import mybir


def conv_bn_relu_program(nc, x, w_bins, w_center, b_center, gamma, beta, out, y_dram):
    F32 = mybir.dt.float32
    F32R = mybir.dt.float32r
    ALU = mybir.AluOpType
    ACT = mybir.ActivationFunctionType

    IMAGES, CHANNELS, H, W = x.shape
    P = 128
    CH = CHANNELS // P
    HW = H * W
    HALF_ROWS = H // 2
    HALF = HALF_ROWS * W
    EPS = 1e-5
    PAIRS = IMAGES // 2
    TAPS = w_bins.shape[1] + 1
    X_TAPS = [(0, 0, 0), (1, 1, 0), (2, 1, -1), (3, -1, 0), (4, -1, 1)]
    V_TAPS = [(5, 0, 1), (6, -1, -1)]
    POOLED = 6
    FIRST_POOLED_TAP = len(X_TAPS) + len(V_TAPS)
    GROUPS = [(0, 5, 1), (5, 7, 2), (7, 9, 14), (9, 13, 11)]
    SPLIT_SLOTS = 4
    SUM_SLOTS = 4
    TAIL = 4
    ROUNDS = IMAGES // TAIL

    x_img = x.rearrange("n (c p) h w -> n p c (h w)", p=P)
    out_img = out.rearrange("n (c p) h w -> n p c (h w)", p=P)
    w_bins_v = w_bins.rearrange("(c p) k o -> p c k o", p=P)
    w_center_v = w_center.rearrange("(c p) o -> p c o", p=P)

    ctx = ExitStack()
    with ctx:
        def sb(name, shape, dt=F32):
            return ctx.enter_context(nc.sbuf_tensor(name, shape, dt))

        def sem(name):
            return ctx.enter_context(nc.semaphore(name))

        w_hi = sb("w_hi", [P, CH, TAPS, CHANNELS], F32R)
        w_lo = sb("w_lo", [P, CH, TAPS, CHANNELS], F32R)
        x_stage = sb("x_stage", [P, CH, H, W])
        x_pad = sb("x_pad", [P, H + 2, W + 4])
        x_hi = sb("x_hi", [P, CH, H + 2, W + 2], F32R)
        x_lo = sb("x_lo", [P, CH, H + 2, W + 2], F32R)
        v_hi = sb("v_hi", [P, CH, H + 1, W + 2], F32R)
        v_lo = sb("v_lo", [P, CH, H + 1, W + 2], F32R)
        row2 = sb("row2", [P, H + 8, W + 8])
        row3 = sb("row3", [P, H + 4, W + 6])
        row3v = sb("row3v", [P, H + 2, W + 2])
        box = sb("box", [P, H + 6, W + 6])
        ends = sb("ends", [P, H + 8, W])
        pooled = sb("pooled", [P, SUM_SLOTS, H, W])
        v_sum = [pooled[:, :, :, :].rearrange("p a h w -> p (a h w)")[:, b:b + (H + 1) * W]
                 .rearrange("p (h w) -> p h w", w=W) for b in (2 * HW, 0)]
        pooled_hi = sb("pooled_hi", [P, SPLIT_SLOTS, H, W], F32R)
        pooled_lo = sb("pooled_lo", [P, SPLIT_SLOTS, H, W], F32R)
        y_stage = sb("y_stage", [P, CH, HW])
        tail = sb("tail", [P, TAIL, 2, CH, HW])
        w_stage = tail[:, :, :, :, :].rearrange("p a b c f -> p (a b c f)")[:, 0:CH * TAPS * CHANNELS]\
            .rearrange("p (c k o) -> p c k o", c=CH, k=TAPS)
        stats = sb("stats", [P, CH, IMAGES * 2, 6])
        moments = sb("moments", [P, CH, 2])
        bias = sb("bias", [P, CH])
        gam = sb("gam", [P, CH])
        bet = sb("bet", [P, CH])
        var = sb("var", [P, CH])
        std = sb("std", [P, CH])
        rstd = sb("rstd", [P, CH])
        newton = sb("newton", [P, CH])
        bn_scale = sb("bn_scale", [P, CH])
        bn_shift = sb("bn_shift", [P, CH])
        acc = ctx.enter_context(nc.psum_tensor("acc", [P, 2, CH, 2, 512], F32))

        params_loaded = sem("params_loaded")
        w_loaded = [sem(f"w_loaded{c}") for c in range(CH)]
        w_hi_ready = sem("w_hi_ready")
        w_lo_ready = sem("w_lo_ready")
        pads_zeroed = sem("pads_zeroed")
        borders_zeroed = sem("borders_zeroed")
        x_loaded = [sem(f"x_loaded{c}") for c in range(CH)]
        x_pad_ready = sem("x_pad_ready")
        x_hi_ready = sem("x_hi_ready")
        x_lo_ready = sem("x_lo_ready")
        x_taps_done = sem("x_taps_done")
        v_sum_ready = sem("v_sum_ready")
        v_hi_ready = sem("v_hi_ready")
        v_lo_ready = sem("v_lo_ready")
        v_taps_done = sem("v_taps_done")
        row2_ready = sem("row2_ready")
        row3_ready = sem("row3_ready")
        row3v_ready = sem("row3v_ready")
        box_ready = sem("box_ready")
        ends_ready = sem("ends_ready")
        part_ready = sem("part_ready")
        pooled_ready = sem("pooled_ready")
        pooled_hi_ready = sem("pooled_hi_ready")
        pooled_lo_ready = sem("pooled_lo_ready")
        pooled_done = sem("pooled_done")
        banks_copied = sem("banks_copied")
        banks_measured = sem("banks_measured")
        y_saved = sem("y_saved")
        bn_chain = sem("bn_chain")
        var_ready = sem("var_ready")
        std_ready = sem("std_ready")
        bn_ready = sem("bn_ready")
        tail_loaded = [sem(f"tail_loaded{d}") for d in range(TAIL)]
        scaled = sem("scaled")
        relu_done = sem("relu_done")
        stored = [sem(f"stored{d}") for d in range(TAIL)]

        def wait_from_one(engine, semaphore, count):
            if isinstance(count, int) and count <= 0:
                return
            engine.wait_ge(semaphore, count)

        block = ctx.enter_context(nc.Block())

        @block.gpsimd
        def _(pool):
            for c in range(CH):
                for plane in (x_hi, x_lo, v_hi, v_lo):
                    nc.gpsimd.memset(plane[:, c].bitcast(F32), 0.0).then_inc(borders_zeroed, 1)

        @block.sync
        def _(sp):
            def load_set(image, c):
                sp.dma_start(x_stage[:, c].rearrange("p h w -> p (h w)"),
                             x_img[bass.ds(image, 1), :, c].rearrange("n p f -> p (n f)"))\
                    .then_inc(x_loaded[c], 16)

            def load_weights(c):
                sp.dma_start(w_stage[:, c, 0, :], w_center_v[:, c, :]).then_inc(w_loaded[c], 16)
                sp.dma_start(w_stage[:, c, 1:TAPS, :], w_bins_v[:, c, :, :]).then_inc(w_loaded[c], 16)

            def save(image):
                sp.wait_ge(banks_copied, image + 1 + 2)
                sp.dma_start(y_dram[bass.ds(image, 1)].rearrange("n p f -> p (n f)"),
                             y_stage[:, :, :].rearrange("p c f -> p (c f)")).then_inc(y_saved, 16)

            def image_steps(image, first=False, last=False):
                if not last:
                    for c in range(CH):
                        sp.wait_ge(x_lo_ready, 2 * image + c + 1)
                        load_set(image + 1, c)
                if not first:
                    save(image - 1)

            def tail_load(round_, d):
                image = round_ * TAIL + d
                sp.dma_start(tail[:, d, 0].rearrange("p c f -> p (c f)"),
                             y_dram[bass.ds(image, 1)].rearrange("n p f -> p (n f)"))\
                    .then_inc(tail_loaded[d], 16)
                sp.dma_start(tail[:, d, 1],
                             x_img[bass.ds(image, 1)].rearrange("n p c f -> p (n c) f"))\
                    .then_inc(tail_loaded[d], 16)

            load_set(0, 0)
            load_weights(0)
            load_set(0, 1)
            load_weights(1)
            for dst, src in ((bias, b_center), (gam, gamma), (bet, beta)):
                sp.dma_start(dst[:, :], src).then_inc(params_loaded, 16)
            image_steps(0, first=True)
            with sp.Fori(1, IMAGES - 2) as image:
                image_steps(image)
            sp.wait_ge(y_saved, 16 * TAIL)
            sp.wait_ge(w_lo_ready, CH * len(GROUPS))
            image_steps(IMAGES - 2)
            for d in range(TAIL):
                tail_load(0, d)
            image_steps(IMAGES - 1, last=True)
            save(IMAGES - 1)
            sp.wait_ge(y_saved, 16 * IMAGES)
            with sp.Fori(1, ROUNDS) as round_:
                for d in range(TAIL):
                    sp.wait_ge(stored[d], 16 * round_)
                    tail_load(round_, d)
            for d in range(TAIL):
                sp.wait_ge(stored[d], 16 * ROUNDS)

        @block.scalar
        def _(act):
            def split_weights(c):
                act.wait_ge(w_loaded[c], 32)
                for a, b, count in GROUPS:
                    nc.scalar.activation(w_hi[:, c, a:b, :], w_stage[:, c, a:b, :], ACT.Copy,
                                         scale=1.0 / count).then_inc(w_hi_ready, 1)

            def spread_x(s, c, image):
                act.wait_ge(x_loaded[c], 16 * (image + 1))
                nc.scalar.activation(x_pad[:, 1:H + 1, 2:W + 2], x_stage[:, c], ACT.Copy)\
                    .then_inc(x_pad_ready, 1)
                wait_from_one(act, x_taps_done, s - 1)
                nc.scalar.activation(x_hi[:, c, 1:H + 1, 1:W + 1], x_stage[:, c], ACT.Copy)\
                    .then_inc(x_hi_ready, 1)

            def split_pooled(n, k):
                wait_from_one(act, pooled_done, n - SPLIT_SLOTS + 1)
                act.wait_ge(pooled_ready, n + 1)
                nc.scalar.activation(pooled_hi[:, k % SPLIT_SLOTS], pooled[:, k % SUM_SLOTS], ACT.Copy)\
                    .then_inc(pooled_hi_ready, 1)

            def copy_banks(image, parity):
                act.wait_ge(pooled_done, 2 * POOLED * (image + 1))
                wait_from_one(act, y_saved, 16 * image)
                for o in range(CH):
                    done = nc.scalar.activation(
                        y_stage[:, o].rearrange("p (a f) -> p a f", a=2),
                        acc[:, parity, o, :, 0:HALF], ACT.Identity, bias=bias[:, o:o + 1])
                done.then_inc(banks_copied, 1)

            def image_steps(image, parity, first=False, last=False):
                for c in range(CH):
                    s = 2 * image + c
                    n = POOLED * s
                    k = POOLED * c
                    wait_from_one(act, v_taps_done, s - 1)
                    act.wait_ge(v_sum_ready, s + 1)
                    if first:
                        act.wait_ge(borders_zeroed, 4 * c + 3)
                    nc.scalar.activation(v_hi[:, c, :, 1:W + 1], v_sum[c], ACT.Copy)\
                        .then_inc(v_hi_ready, 1)
                    split_pooled(n, k)
                    split_pooled(n + 1, k + 1)
                    if not (last and c == CH - 1):
                        if first and c == 0:
                            act.wait_ge(borders_zeroed, 5)
                        spread_x(s + 1, 1 - c, image + c)
                    for m in range(2, POOLED):
                        split_pooled(n + m, k + m)
                    if c == 0 and not first:
                        copy_banks(image - 1, 1 - parity)

            act.sem_inc(banks_copied, 2)
            split_weights(0)
            act.wait_ge(pads_zeroed, 1)
            act.wait_ge(borders_zeroed, 1)
            spread_x(0, 0, 0)
            split_weights(1)
            act.wait_ge(params_loaded, 48)
            image_steps(0, 0, first=True)
            image_steps(1, 1)
            with act.Fori(1, PAIRS - 1) as pair:
                image_steps(2 * pair, 0)
                image_steps(2 * pair + 1, 1)
            image_steps(IMAGES - 2, 0)
            image_steps(IMAGES - 1, 1, last=True)
            copy_banks(IMAGES - 1, 1)

            act.wait_ge(var_ready, 1)
            nc.scalar.activation(std[:, :], var[:, :], ACT.Sqrt).then_inc(std_ready, 1)
            act.wait_ge(bn_ready, 1)
            with act.Fori(0, ROUNDS) as round_:
                for d in range(TAIL):
                    image = round_ * TAIL + d
                    for o in range(CH):
                        act.wait_ge(scaled, CH * image + o + 1)
                        nc.scalar.activation(tail[:, d, 0, o], tail[:, d, 0, o], ACT.Relu,
                                             bias=bn_shift[:, o:o + 1]).then_inc(relu_done, 1)
                    act.wait_ge(relu_done, CH * (image + 1))
                    act.dma_start(out_img[bass.ds(image, 1)].rearrange("n p c f -> p (n c) f"),
                                  tail[:, d, 0]).then_inc(stored[d], 16)

        @block.vector
        def _(dve):
            add = lambda out_, a, b: nc.vector.tensor_tensor(out_, a, b, ALU.add)
            sub = lambda out_, a, b: nc.vector.tensor_tensor(out_, a, b, ALU.subtract)

            def split_weights(c):
                for g, (a, b, count) in enumerate(GROUPS):
                    dve.wait_ge(w_hi_ready, c * len(GROUPS) + g + 1)
                    nc.vector.scalar_tensor_tensor(
                        out=w_lo[:, c, a:b, :].rearrange("p k o -> p (k o)"),
                        in0=w_stage[:, c, a:b, :].rearrange("p k o -> p (k o)"), scalar=1.0 / count,
                        in1=w_hi[:, c, a:b, :].bitcast(F32).rearrange("p k o -> p (k o)"),
                        op0=ALU.mult, op1=ALU.subtract).then_inc(w_lo_ready, 1)

            def box_at(dy, dx):
                return box[:, 3 + dy:3 + dy + H, 3 + dx:3 + dx + W]

            def row3_at(dx):
                return row3[:, 2:2 + H, 3 + dx:3 + dx + W]

            def row2_at(dy, dx):
                return row2[:, 4 + dy:4 + dy + H, 4 + dx:4 + dx + W]

            def ends_at(dy):
                return ends[:, 4 + dy:4 + dy + H, :]

            def lo_of_pooled(n, k):
                dve.wait_ge(pooled_hi_ready, n + 1)
                sub(pooled_lo[:, k % SPLIT_SLOTS], pooled[:, k % SUM_SLOTS],
                    pooled_hi[:, k % SPLIT_SLOTS].bitcast(F32)).then_inc(pooled_lo_ready, 1)

            def measure(image, parity):
                dve.wait_ge(banks_copied, image + 1 + 2)
                for o in range(CH):
                    for half in range(2):
                        done = nc.vector.bn_stats(
                            stats[:, o, bass.ds(2 * image + half, 1), :].rearrange("p a b -> p (a b)"),
                            acc[:, parity, o, half, 0:HALF])
                done.then_inc(banks_measured, 1)

            def image_steps(image, parity, first=False):
                for c in range(CH):
                    s = 2 * image + c
                    n = POOLED * s
                    k = POOLED * c

                    def sum_slot(m):
                        return pooled[:, (k + m) % SUM_SLOTS]

                    def first_sum(m, a, b):
                        if m == 2:
                            dve.wait_ge(v_lo_ready, s + 1)
                        wait_from_one(dve, pooled_lo_ready, n + m - SUM_SLOTS + 1)
                        return add(sum_slot(m), a, b)

                    wait_from_one(dve, pooled_ready, n)
                    dve.wait_ge(x_pad_ready, s + 1)
                    add(row2[:, 4:4 + H, 3:4 + W], x_pad[:, 1:1 + H, 1:2 + W],
                        x_pad[:, 1:1 + H, 2:3 + W]).then_inc(row2_ready, 1)
                    dve.wait_ge(x_hi_ready, s + 1)
                    if first:
                        dve.wait_ge(borders_zeroed, 4 * c + 2)
                    sub(x_lo[:, c, 1:H + 1, 1:W + 1], x_stage[:, c],
                        x_hi[:, c, 1:H + 1, 1:W + 1].bitcast(F32)).then_inc(x_lo_ready, 1)
                    wait_from_one(dve, pooled_lo_ready, n)
                    add(v_sum[c], x_pad[:, 0:H + 1, 2:2 + W],
                        x_pad[:, 1:H + 2, 2:2 + W]).then_inc(v_sum_ready, 1)
                    dve.wait_ge(row2_ready, s + 1)
                    add(row3[:, 2:2 + H, 2:4 + W], row2[:, 4:4 + H, 2:4 + W],
                        x_pad[:, 1:1 + H, 2:4 + W]).then_inc(row3_ready, 1)
                    add(ends[:, 4:4 + H, :], x_pad[:, 1:1 + H, 0:W],
                        x_pad[:, 1:1 + H, 4:4 + W]).then_inc(ends_ready, 1)
                    dve.wait_ge(row3_ready, s + 1)
                    add(row3v[:, 1:2 + H, :], row3[:, 1:2 + H, 2:4 + W],
                        row3[:, 2:3 + H, 2:4 + W]).then_inc(row3v_ready, 1)
                    dve.wait_ge(v_hi_ready, s + 1)
                    if first:
                        dve.wait_ge(borders_zeroed, 4 * c + 4)
                    sub(v_lo[:, c, :, 1:W + 1], v_sum[c],
                        v_hi[:, c, :, 1:W + 1].bitcast(F32)).then_inc(v_lo_ready, 1)
                    dve.wait_ge(row3v_ready, s + 1)
                    add(box[:, 2:4 + H, 2:4 + W], row3v[:, 0:2 + H, :],
                        row3[:, 2:4 + H, 2:4 + W]).then_inc(box_ready, 1)
                    if c == 1 and not first:
                        measure(image - 1, 1 - parity)
                    dve.wait_ge(box_ready, s + 1)
                    first_sum(0, box_at(-2, -3), row3_at(-3)).then_inc(part_ready, 1)
                    first_sum(1, box_at(2, 3), row3_at(3)).then_inc(part_ready, 1)
                    dve.wait_ge(part_ready, 2 * s + 1)
                    add(sum_slot(0)[:, 4:H, 3:W], sum_slot(0)[:, 4:H, 3:W],
                        row2[:, 4:H, 3:W]).then_inc(pooled_ready, 1)
                    dve.wait_ge(part_ready, 2 * s + 2)
                    add(sum_slot(1)[:, 0:H - 4, 0:W - 3], sum_slot(1)[:, 0:H - 4, 0:W - 3],
                        row2[:, 8:4 + H, 7:4 + W]).then_inc(pooled_ready, 1)
                    first_sum(2, box_at(-2, 3), row2_at(-4, 3)).then_inc(pooled_ready, 1)
                    lo_of_pooled(n, k)
                    first_sum(3, box_at(2, -3), row2_at(4, -4)).then_inc(pooled_ready, 1)
                    lo_of_pooled(n + 1, k + 1)
                    dve.wait_ge(ends_ready, s + 1)
                    first_sum(4, box_at(3, 0), ends_at(4)).then_inc(pooled_ready, 1)
                    lo_of_pooled(n + 2, k + 2)
                    first_sum(5, box_at(-3, 0), ends_at(-4)).then_inc(pooled_ready, 1)
                    for m in range(3, POOLED):
                        lo_of_pooled(n + m, k + m)

            dve.sem_inc(banks_measured, 2)
            nc.vector.memset(x_pad[:, :, :], 0.0).then_inc(pads_zeroed, 1)
            nc.vector.memset(row2[:, :, :], 0.0).then_inc(pads_zeroed, 1)
            nc.vector.memset(row3[:, :, :], 0.0).then_inc(pads_zeroed, 1)
            nc.vector.memset(row3v[:, 0:1, :], 0.0).then_inc(pads_zeroed, 1)
            nc.vector.memset(box[:, :, :], 0.0).then_inc(pads_zeroed, 1)
            nc.vector.memset(ends[:, 0:4, :], 0.0).then_inc(pads_zeroed, 1)
            nc.vector.memset(ends[:, 4 + H:8 + H, :], 0.0).then_inc(pads_zeroed, 1)
            split_weights(0)
            dve.wait_ge(pads_zeroed, 7)
            split_weights(1)
            image_steps(0, 0, first=True)
            image_steps(1, 1)
            with dve.Fori(1, PAIRS) as pair:
                image_steps(2 * pair, 0)
                image_steps(2 * pair + 1, 1)
            measure(IMAGES - 1, 1)

            chain = [0]

            def link(ins):
                chain[0] += 1
                ins.then_inc(bn_chain, 1)
                dve.wait_ge(bn_chain, chain[0])

            dve.wait_ge(banks_measured, IMAGES + 2)
            for o in range(CH):
                link(nc.vector.bn_aggr(moments[:, o, :], stats[:, o].rearrange("p a b -> p (a b)")))
            dve.wait_ge(params_loaded, 48)
            nc.vector.tensor_scalar(var[:, :], moments[:, :, 1], EPS, None, ALU.add).then_inc(var_ready, 1)
            link(add(moments[:, :, 0], moments[:, :, 0], bias[:, :]))
            dve.wait_ge(std_ready, 1)
            link(nc.vector.reciprocal(rstd[:, :], std[:, :]))
            link(nc.vector.tensor_tensor(newton[:, :], rstd[:, :], rstd[:, :], ALU.mult))
            link(nc.vector.tensor_tensor(newton[:, :], newton[:, :], var[:, :], ALU.mult))
            link(nc.vector.tensor_scalar(newton[:, :], newton[:, :], -0.5, 1.5, ALU.mult, ALU.add))
            link(nc.vector.tensor_tensor(rstd[:, :], rstd[:, :], newton[:, :], ALU.mult))
            link(nc.vector.tensor_tensor(bn_scale[:, :], rstd[:, :], gam[:, :], ALU.mult))
            link(nc.vector.tensor_tensor(newton[:, :], moments[:, :, 0], bn_scale[:, :], ALU.mult))
            sub(bn_shift[:, :], bet[:, :], newton[:, :]).then_inc(bn_ready, 1)

            with dve.Fori(0, ROUNDS) as round_:
                for d in range(TAIL):
                    dve.wait_ge(tail_loaded[d], 32 * round_ + 32)
                    for o in range(CH):
                        nc.vector.scalar_tensor_tensor(
                            out=tail[:, d, 0, o], in0=tail[:, d, 0, o], scalar=bn_scale[:, o:o + 1],
                            in1=tail[:, d, 1, o], op0=ALU.mult, op1=ALU.add).then_inc(scaled, 1)

        @block.tensor
        def _(pe):
            def products(parity, c, tap, hi, lo, window, start, stop):
                for o in range(CH):
                    cols = slice(o * P, (o + 1) * P)
                    for half in range(2):
                        bank = acc[:, parity, o, half, 0:HALF].rearrange("p (h w) -> p h w", w=W)
                        nc.tensor.matmul(bank, w_hi[:, c, tap, cols], window(hi, half),
                                         start=start, stop=False)
                        nc.tensor.matmul(bank, w_lo[:, c, tap, cols], window(hi, half),
                                         start=False, stop=False)
                        last = nc.tensor.matmul(bank, w_hi[:, c, tap, cols], window(lo, half),
                                                start=False, stop=stop)
                return last

            def shifted(row, col):
                return lambda plane, half: plane[:, half * HALF_ROWS + row:half * HALF_ROWS + row + HALF_ROWS,
                                                 col:col + W]

            pe.wait_ge(w_lo_ready, len(GROUPS))
            with pe.Fori(0, PAIRS) as pair:
                for parity in range(2):
                    pe.wait_ge(banks_copied, 2 * pair + parity + 1)
                    pe.wait_ge(banks_measured, 2 * pair + parity + 1)
                    for c in range(CH):
                        s = 4 * pair + 2 * parity + c
                        if c == 1:
                            pe.wait_ge(w_lo_ready, CH * len(GROUPS))
                        pe.wait_ge(x_lo_ready, s + 1)
                        for i, (tap, dy, dx) in enumerate(X_TAPS):
                            last = products(parity, c, tap, x_hi[:, c], x_lo[:, c], shifted(1 + dy, 1 + dx),
                                            start=(c == 0 and i == 0), stop=False)
                        last.then_inc(x_taps_done, 1)
                        pe.wait_ge(v_lo_ready, s + 1)
                        for tap, dy, dx in V_TAPS:
                            last = products(parity, c, tap, v_hi[:, c], v_lo[:, c], shifted(1 + dy, 1 + dx),
                                            start=False, stop=False)
                        last.then_inc(v_taps_done, 1)
                        for m in range(POOLED):
                            slot = (POOLED * c + m) % SPLIT_SLOTS
                            pe.wait_ge(pooled_lo_ready, POOLED * s + m + 1)
                            products(parity, c, FIRST_POOLED_TAP + m, pooled_hi[:, slot], pooled_lo[:, slot],
                                     shifted(0, 0), start=False, stop=(c == CH - 1 and m == POOLED - 1))\
                                .then_inc(pooled_done, 1)


def kernel(x, L0_conv_w_conv1, L0_conv_w_center, L0_conv_b_center, L0_conv_gamma, L0_conv_beta):
    import numpy as np
    import concourse.bacc as bacc
    from concourse import mybir
    from concourse.bass_utils import run_bass_kernel_spmd

    images, channels, height, width = x.shape
    order = [1, 2, 4, 5, 0, 3, 9, 6, 11, 8, 7, 10]
    w = np.asarray(L0_conv_w_conv1)
    bins = w.shape[2] * w.shape[3]
    w_bins = np.ascontiguousarray(w.reshape(channels, channels, bins).transpose(1, 2, 0)[:, order, :])
    w_center = np.ascontiguousarray(np.asarray(L0_conv_w_center).reshape(channels, channels).transpose(1, 0))

    def per_partition(v):
        return np.ascontiguousarray(np.asarray(v).reshape(-1, 128).T)

    arrays = {
        "x": np.ascontiguousarray(x),
        "w_bins": w_bins,
        "w_center": w_center,
        "b_center": per_partition(L0_conv_b_center),
        "gamma": per_partition(L0_conv_gamma),
        "beta": per_partition(L0_conv_beta),
    }
    nc = bacc.Bacc("TRN2", target_bir_lowering=False, num_devices=1)
    f32 = mybir.dt.float32
    args = [nc.dram_tensor(name, a.shape, f32, kind="ExternalInput").ap() for name, a in arrays.items()]
    out = nc.dram_tensor("out", (images, channels, height, width), f32, kind="ExternalOutput").ap()
    y_dram = nc.dram_tensor("y_dram", (images, 128, channels // 128 * height * width), f32,
                            kind="Internal").ap()
    conv_bn_relu_program(nc, *args, out, y_dram)
    result = run_bass_kernel_spmd(nc, [arrays], core_ids=[0])
    return result.results[0]["out"]
```

```python
from contextlib import ExitStack

import concourse.bass as bass
from concourse import mybir


def conv_bn_relu_program(nc, x, w_bins, w_center, b_center, gamma, beta, out, y_dram):
    F32 = mybir.dt.float32
    F32R = mybir.dt.float32r
    ALU = mybir.AluOpType
    ACT = mybir.ActivationFunctionType

    IMAGES, CHANNELS, H, W = x.shape
    P = 128
    CH = CHANNELS // P
    HW = H * W
    HALF_ROWS = H // 2
    HALF = HALF_ROWS * W
    EPS = 1e-5
    PAIRS = IMAGES // 2
    TAPS = w_bins.shape[1] + 1
    X_TAPS = [(0, 0, 0), (1, 1, 0), (2, 1, -1), (3, -1, 0), (4, -1, 1)]
    V_TAPS = [(5, 0, 1), (6, -1, -1)]
    PLANES = [((0, H), (2, W)),
              ((0, H), (0, W - 2)),
              ((1, H), (0, W - 2)),
              ((0, H - 1), (2, W)),
              ((0, H - 2), (0, W)),
              ((2, H), (0, W))]
    POOLED = len(PLANES)
    FIRST_POOLED_TAP = len(X_TAPS) + len(V_TAPS)
    GROUPS = [(0, 5, 1), (5, 7, 2), (7, 9, 14), (9, 13, 11)]
    SPLIT_SLOTS = 4
    SUM_SLOTS = 4
    TAIL = 8
    RING = 5
    ROUNDS = IMAGES // TAIL

    x_img = x.rearrange("n (c p) h w -> n p c (h w)", p=P)
    out_img = out.rearrange("n (c p) h w -> n p c (h w)", p=P)
    w_bins_v = w_bins.rearrange("(c p) k o -> p c k o", p=P)
    w_center_v = w_center.rearrange("(c p) o -> p c o", p=P)

    ctx = ExitStack()
    with ctx:
        def sb(name, shape, dt=F32):
            return ctx.enter_context(nc.sbuf_tensor(name, shape, dt))

        def sem(name):
            return ctx.enter_context(nc.semaphore(name))

        w_hi = [None, sb("w_hi1", [P, TAPS, CHANNELS], F32R)]
        w_lo = [None, sb("w_lo1", [P, TAPS, CHANNELS], F32R)]
        with ExitStack() as first_half:
            w_hi[0] = first_half.enter_context(nc.sbuf_tensor("w_hi0", [P, TAPS, CHANNELS], F32R))
            w_lo[0] = first_half.enter_context(nc.sbuf_tensor("w_lo0", [P, TAPS, CHANNELS], F32R))
        late = sb("late", [P, 2, TAPS * CHANNELS])
        x_stage = sb("x_stage", [P, CH, HW])
        x_pad = sb("x_pad", [P, H + 2, W + 4])
        x_hi = sb("x_hi", [P, CH, H, W + 2], F32R)
        x_lo = sb("x_lo", [P, CH, H, W + 2], F32R)
        v_hi = sb("v_hi", [P, H + 1, W + 2], F32R)
        v_lo = sb("v_lo", [P, H + 1, W + 2], F32R)
        row2 = sb("row2", [P, H + 6, W + 3])
        row3 = sb("row3", [P, H + 3, W + 2])
        row3v = sb("row3v", [P, H + 2, W + 2])
        box = sb("box", [P, H + 4, W + 2])
        ends = sb("ends", [P, H + 4, W])
        pooled = sb("pooled", [P, SUM_SLOTS, HW])
        v_sum = [pooled[:, :, :].rearrange("p a f -> p (a f)")[:, b:b + (H + 1) * W]
                 .rearrange("p (h w) -> p h w", w=W) for b in (2 * HW, 0)]
        pooled_hi = sb("pooled_hi", [P, SPLIT_SLOTS, HW], F32R)
        pooled_lo = sb("pooled_lo", [P, SPLIT_SLOTS, HW], F32R)
        y_stage = sb("y_stage", [P, CH, HW])
        tail = sb("tail", [P, RING, 2, CH, HW])
        w_stage = tail[:, :, :, :, :].rearrange("p a b c f -> p (a b c f)")[:, 0:CH * TAPS * CHANNELS]\
            .rearrange("p (c k o) -> p c k o", c=CH, k=TAPS)

        def late_slot(k):
            both = late[:, k, 0:2 * CH * HW].rearrange("p (b c f) -> p b c f", b=2, c=CH)
            return both[:, 0], both[:, 1]

        slots = [(y_stage, x_stage)] + [(tail[:, d, 0], tail[:, d, 1]) for d in range(RING)]\
            + [late_slot(0), late_slot(1)]
        assert len(slots) == TAIL and IMAGES % TAIL == 0
        stats = sb("stats", [P, CH, IMAGES * 2, 6])
        moments = sb("moments", [P, CH, 2])
        bias = sb("bias", [P, CH])
        gam = sb("gam", [P, CH])
        bet = sb("bet", [P, CH])
        var = sb("var", [P, CH])
        std = sb("std", [P, CH])
        rstd = sb("rstd", [P, CH])
        newton = sb("newton", [P, CH])
        bn_scale = sb("bn_scale", [P, CH])
        bn_shift = sb("bn_shift", [P, CH])
        acc = ctx.enter_context(nc.psum_tensor("acc", [P, 2, CH, 2, 512], F32))

        params_loaded = sem("params_loaded")
        w_loaded = [[sem(f"w_loaded{c}{g}") for g in range(len(GROUPS))] for c in range(CH)]
        w_hi_ready = sem("w_hi_ready")
        w_lo_ready = sem("w_lo_ready")
        pads_zeroed = sem("pads_zeroed")
        borders_zeroed = sem("borders_zeroed")
        x_loaded = [sem(f"x_loaded{c}") for c in range(CH)]
        x_pad_ready = sem("x_pad_ready")
        x_hi_ready = sem("x_hi_ready")
        x_lo_ready = sem("x_lo_ready")
        x_taps_done = sem("x_taps_done")
        v_sum_ready = sem("v_sum_ready")
        v_hi_ready = sem("v_hi_ready")
        v_lo_ready = sem("v_lo_ready")
        v_taps_done = sem("v_taps_done")
        row2_ready = sem("row2_ready")
        row3_ready = sem("row3_ready")
        row3v_ready = sem("row3v_ready")
        box_ready = sem("box_ready")
        ends_ready = sem("ends_ready")
        part_ready = sem("part_ready")
        pooled_ready = sem("pooled_ready")
        pooled_hi_ready = sem("pooled_hi_ready")
        pooled_lo_ready = sem("pooled_lo_ready")
        pooled_done = sem("pooled_done")
        banks_copied = sem("banks_copied")
        banks_measured = sem("banks_measured")
        y_saved = sem("y_saved")
        bn_chain = sem("bn_chain")
        var_ready = sem("var_ready")
        std_ready = sem("std_ready")
        bn_ready = sem("bn_ready")
        tail_loaded = [sem(f"tail_loaded{d}") for d in range(TAIL)]
        scaled = sem("scaled")
        relu_done = sem("relu_done")
        stored = [sem(f"stored{d}") for d in range(TAIL)]

        def wait_from_one(engine, semaphore, count):
            if isinstance(count, int) and count <= 0:
                return
            engine.wait_ge(semaphore, count)

        def plane_size(m):
            (r0, r1), (c0, c1) = PLANES[m]
            return (r1 - r0) * (c1 - c0)

        def tail_image(round_, d):
            return TAIL * round_ + d - 1

        block = ctx.enter_context(nc.Block())

        @block.gpsimd
        def _(pool):
            for plane in (x_hi[:, 0], x_lo[:, 0], v_hi, v_lo, x_hi[:, 1], x_lo[:, 1]):
                nc.gpsimd.memset(plane[:, :, 0:W + 2:W + 1].bitcast(F32), 0.0).then_inc(borders_zeroed, 1)

        @block.sync
        def _(sp):
            def load_set(image, c):
                sp.dma_start(x_stage[:, c],
                             x_img[bass.ds(image, 1), :, c].rearrange("n p f -> p (n f)"))\
                    .then_inc(x_loaded[c], 16)

            def load_weights(c):
                for g, (a, b, _) in enumerate(GROUPS):
                    if g == 0:
                        sp.dma_start(w_stage[:, c, 0, :], w_center_v[:, c, :]).then_inc(w_loaded[c][g], 16)
                    a = max(a, 1)
                    sp.dma_start(w_stage[:, c, a:b, :], w_bins_v[:, c, a - 1:b - 1, :])\
                        .then_inc(w_loaded[c][g], 16)

            def save(image):
                sp.wait_ge(banks_copied, image + 1 + 2)
                sp.dma_start(y_dram[bass.ds(image, 1)].rearrange("n p f -> p (n f)"),
                             y_stage[:, :, :].rearrange("p c f -> p (c f)")).then_inc(y_saved, 16)

            def image_steps(image, first=False, last=False):
                if not last:
                    for c in range(CH):
                        sp.wait_ge(x_lo_ready, 2 * image + c + 1)
                        load_set(image + 1, c)
                if not first:
                    save(image - 1)

            def tail_load(round_, d):
                y_slot, x_slot = slots[d]
                image = tail_image(round_, d)
                sp.dma_start(y_slot[:, :, :].rearrange("p c f -> p (c f)"),
                             y_dram[bass.ds(image, 1)].rearrange("n p f -> p (n f)"))\
                    .then_inc(tail_loaded[d], 16)
                sp.dma_start(x_slot[:, :, :],
                             x_img[bass.ds(image, 1)].rearrange("n p c f -> p (n c) f"))\
                    .then_inc(tail_loaded[d], 16)

            load_set(0, 0)
            load_weights(0)
            load_set(0, 1)
            load_weights(1)
            for dst, src in ((bias, b_center), (gam, gamma), (bet, beta)):
                sp.dma_start(dst[:, :], src).then_inc(params_loaded, 16)
            image_steps(0, first=True)
            with sp.Fori(1, IMAGES - 2) as image:
                image_steps(image)
            image_steps(IMAGES - 2)
            sp.wait_ge(y_saved, 16 * TAIL)
            sp.wait_ge(w_lo_ready, CH * len(GROUPS))
            for d in range(1, 1 + RING):
                tail_load(0, d)
            image_steps(IMAGES - 1, last=True)
            sp.wait_ge(pooled_done, POOLED * (2 * IMAGES - 1))
            for d in range(1 + RING, TAIL):
                tail_load(0, d)
            sp.wait_ge(y_saved, 16 * (IMAGES - 1))
            with sp.Fori(1, ROUNDS) as round_:
                for d in range(TAIL):
                    sp.wait_ge(stored[d], 16 * round_)
                    tail_load(round_, d)
            for d in range(TAIL):
                sp.wait_ge(stored[d], 16 * ROUNDS)

        @block.scalar
        def _(act):
            def split_weights(c, groups):
                for g in groups:
                    a, b, count = GROUPS[g]
                    act.wait_ge(w_loaded[c][g], 32 if g == 0 else 16)
                    nc.scalar.activation(w_hi[c][:, a:b, :], w_stage[:, c, a:b, :], ACT.Copy,
                                         scale=1.0 / count).then_inc(w_hi_ready, 1)

            def spread_x(s, c, image):
                act.wait_ge(x_loaded[c], 16 * (image + 1))
                x_in = x_stage[:, c].rearrange("p (h w) -> p h w", w=W)
                nc.scalar.activation(x_pad[:, 1:H + 1, 2:W + 2], x_in, ACT.Copy).then_inc(x_pad_ready, 1)
                wait_from_one(act, x_taps_done, s - 1)
                nc.scalar.activation(x_hi[:, c, :, 1:W + 1], x_in, ACT.Copy).then_inc(x_hi_ready, 1)

            def split_pooled(n, k):
                size = plane_size(k % POOLED)
                wait_from_one(act, pooled_done, n - SPLIT_SLOTS + 1)
                act.wait_ge(pooled_ready, n + 1)
                nc.scalar.activation(pooled_hi[:, k % SPLIT_SLOTS, 0:size], pooled[:, k % SUM_SLOTS, 0:size],
                                     ACT.Copy).then_inc(pooled_hi_ready, 1)

            def copy_banks(image, parity):
                act.wait_ge(pooled_done, 2 * POOLED * (image + 1))
                wait_from_one(act, y_saved, 16 * image)
                for o in range(CH):
                    done = nc.scalar.activation(
                        y_stage[:, o].rearrange("p (a f) -> p a f", a=2),
                        acc[:, parity, o, :, 0:HALF], ACT.Identity, bias=bias[:, o:o + 1])
                done.then_inc(banks_copied, 1)

            def image_steps(image, parity, first=False, last=False):
                for c in range(CH):
                    s = 2 * image + c
                    n = POOLED * s
                    k = POOLED * c
                    wait_from_one(act, v_taps_done, s)
                    act.wait_ge(v_sum_ready, s + 1)
                    if first and c == 0:
                        act.wait_ge(borders_zeroed, 3)
                    nc.scalar.activation(v_hi[:, :, 1:W + 1], v_sum[c], ACT.Copy)\
                        .then_inc(v_hi_ready, 1)
                    split_pooled(n, k)
                    split_pooled(n + 1, k + 1)
                    if first and c == 0:
                        split_weights(1, range(len(GROUPS)))
                    if not (last and c == CH - 1):
                        if first and c == 0:
                            act.wait_ge(borders_zeroed, 5)
                        spread_x(s + 1, 1 - c, image + c)
                    for m in range(2, POOLED):
                        split_pooled(n + m, k + m)
                    if c == 0 and not first:
                        copy_banks(image - 1, 1 - parity)

            def store(round_, d):
                image = IMAGES - 1 if isinstance(round_, int) and d == 0 else tail_image(round_, d)
                act.dma_start(out_img[bass.ds(image, 1)].rearrange("n p c f -> p (n c) f"),
                              slots[d][0][:, :, :]).then_inc(stored[d], 16)

            def tail_round(round_):
                for d in range(TAIL):
                    turn = round_ * TAIL + d
                    y_slot = slots[d][0]
                    for o in range(CH):
                        act.wait_ge(scaled, CH * turn + o + 1)
                        nc.scalar.activation(y_slot[:, o], y_slot[:, o], ACT.Relu,
                                             bias=bn_shift[:, o:o + 1]).then_inc(relu_done, 1)
                    act.wait_ge(relu_done, CH * (turn + 1))
                    store(round_, d)

            act.sem_inc(banks_copied, 2)
            split_weights(0, [0])
            act.wait_ge(pads_zeroed, 1)
            act.wait_ge(borders_zeroed, 1)
            spread_x(0, 0, 0)
            split_weights(0, range(1, len(GROUPS)))
            act.wait_ge(params_loaded, 48)
            image_steps(0, 0, first=True)
            image_steps(1, 1)
            with act.Fori(1, PAIRS - 1) as pair:
                image_steps(2 * pair, 0)
                image_steps(2 * pair + 1, 1)
            image_steps(IMAGES - 2, 0)
            image_steps(IMAGES - 1, 1, last=True)
            copy_banks(IMAGES - 1, 1)

            act.wait_ge(var_ready, 1)
            nc.scalar.activation(std[:, :], var[:, :], ACT.Sqrt).then_inc(std_ready, 1)
            act.wait_ge(bn_ready, 1)
            tail_round(0)
            with act.Fori(1, ROUNDS) as round_:
                tail_round(round_)

        @block.vector
        def _(dve):
            add = lambda out_, a, b: nc.vector.tensor_tensor(out_, a, b, ALU.add)
            sub = lambda out_, a, b: nc.vector.tensor_tensor(out_, a, b, ALU.subtract)

            def split_weights(c, groups):
                for g in groups:
                    a, b, count = GROUPS[g]
                    dve.wait_ge(w_hi_ready, c * len(GROUPS) + g + 1)
                    nc.vector.scalar_tensor_tensor(
                        out=w_lo[c][:, a:b, :].rearrange("p k o -> p (k o)"),
                        in0=w_stage[:, c, a:b, :].rearrange("p k o -> p (k o)"), scalar=1.0 / count,
                        in1=w_hi[c][:, a:b, :].bitcast(F32).rearrange("p k o -> p (k o)"),
                        op0=ALU.mult, op1=ALU.subtract).then_inc(w_lo_ready, 1)

            def piece(source, top, left, m, dy, dx):
                (r0, r1), (c0, c1) = PLANES[m]
                return source[:, r0 + dy - top:r1 + dy - top, c0 + dx - left:c1 + dx - left]

            def box_at(m, dy, dx):
                return piece(box, -2, -1, m, dy, dx)

            def row3_at(m, dx):
                return piece(row3, -1, -1, m, 0, dx)

            def row2_at(m, dy, dx):
                return piece(row2, -3, -2, m, dy, dx)

            def ends_at(m, dy):
                return piece(ends, -2, 0, m, dy, 0)

            def lo_of_pooled(n, k):
                size = plane_size(k % POOLED)
                dve.wait_ge(pooled_hi_ready, n + 1)
                sub(pooled_lo[:, k % SPLIT_SLOTS, 0:size], pooled[:, k % SUM_SLOTS, 0:size],
                    pooled_hi[:, k % SPLIT_SLOTS, 0:size].bitcast(F32)).then_inc(pooled_lo_ready, 1)

            def measure(image, parity):
                dve.wait_ge(banks_copied, image + 1 + 2)
                for o in range(CH):
                    for half in range(2):
                        done = nc.vector.bn_stats(
                            stats[:, o, bass.ds(2 * image + half, 1), :].rearrange("p a b -> p (a b)"),
                            acc[:, parity, o, half, 0:HALF])
                done.then_inc(banks_measured, 1)

            def image_steps(image, parity, first=False):
                for c in range(CH):
                    s = 2 * image + c
                    n = POOLED * s
                    k = POOLED * c

                    def sum_slot(m):
                        (r0, r1), (c0, c1) = PLANES[m]
                        return pooled[:, (k + m) % SUM_SLOTS, 0:plane_size(m)]\
                            .rearrange("p (h w) -> p h w", w=c1 - c0)

                    def first_sum(m, a, b):
                        if m == 2:
                            dve.wait_ge(v_lo_ready, s + 1)
                        wait_from_one(dve, pooled_lo_ready, n + m - SUM_SLOTS + 1)
                        return add(sum_slot(m), a, b)

                    wait_from_one(dve, pooled_ready, n)
                    dve.wait_ge(x_pad_ready, s + 1)
                    add(row2[:, 3:3 + H, 1:2 + W], x_pad[:, 1:1 + H, 1:2 + W],
                        x_pad[:, 1:1 + H, 2:3 + W]).then_inc(row2_ready, 1)
                    dve.wait_ge(x_hi_ready, s + 1)
                    if first:
                        dve.wait_ge(borders_zeroed, 4 * c + 2)
                    sub(x_lo[:, c, :, 1:W + 1], x_stage[:, c].rearrange("p (h w) -> p h w", w=W),
                        x_hi[:, c, :, 1:W + 1].bitcast(F32)).then_inc(x_lo_ready, 1)
                    wait_from_one(dve, pooled_lo_ready, n)
                    add(v_sum[c], x_pad[:, 0:H + 1, 2:2 + W],
                        x_pad[:, 1:H + 2, 2:2 + W]).then_inc(v_sum_ready, 1)
                    dve.wait_ge(row2_ready, s + 1)
                    add(row3[:, 1:1 + H, :], row2[:, 3:3 + H, 0:2 + W],
                        x_pad[:, 1:1 + H, 2:4 + W]).then_inc(row3_ready, 1)
                    if first and c == 0:
                        split_weights(0, [1])
                    add(ends[:, 2:2 + H, :], x_pad[:, 1:1 + H, 0:W],
                        x_pad[:, 1:1 + H, 4:4 + W]).then_inc(ends_ready, 1)
                    dve.wait_ge(row3_ready, s + 1)
                    add(row3v[:, 1:2 + H, :], row3[:, 0:1 + H, :], row3[:, 1:2 + H, :])\
                        .then_inc(row3v_ready, 1)
                    dve.wait_ge(v_hi_ready, s + 1)
                    if first and c == 0:
                        dve.wait_ge(borders_zeroed, 4)
                    sub(v_lo[:, :, 1:W + 1], v_sum[c], v_hi[:, :, 1:W + 1].bitcast(F32))\
                        .then_inc(v_lo_ready, 1)
                    if first and c == 0:
                        split_weights(0, [2, 3])
                    dve.wait_ge(row3v_ready, s + 1)
                    add(box[:, 1:3 + H, :], row3v[:, 0:2 + H, :], row3[:, 1:3 + H, :])\
                        .then_inc(box_ready, 1)
                    if c == 1 and not first:
                        measure(image - 1, 1 - parity)
                    dve.wait_ge(box_ready, s + 1)
                    first_sum(0, box_at(0, -2, -3), row3_at(0, -3)).then_inc(part_ready, 1)
                    first_sum(1, box_at(1, 2, 3), row3_at(1, 3)).then_inc(part_ready, 1)
                    dve.wait_ge(part_ready, 2 * s + 1)
                    corner = sum_slot(0)[:, 4:H, 1:W - 2]
                    add(corner, corner, row2[:, 3:H - 1, 1:W - 2]).then_inc(pooled_ready, 1)
                    dve.wait_ge(part_ready, 2 * s + 2)
                    corner = sum_slot(1)[:, 0:H - 4, 0:W - 3]
                    add(corner, corner, row2[:, 7:3 + H, 5:2 + W]).then_inc(pooled_ready, 1)
                    first_sum(2, box_at(2, -2, 3), row2_at(2, -4, 3)).then_inc(pooled_ready, 1)
                    lo_of_pooled(n, k)
                    first_sum(3, box_at(3, 2, -3), row2_at(3, 4, -4)).then_inc(pooled_ready, 1)
                    lo_of_pooled(n + 1, k + 1)
                    dve.wait_ge(ends_ready, s + 1)
                    first_sum(4, box_at(4, 3, 0), ends_at(4, 4)).then_inc(pooled_ready, 1)
                    lo_of_pooled(n + 2, k + 2)
                    first_sum(5, box_at(5, -3, 0), ends_at(5, -4)).then_inc(pooled_ready, 1)
                    for m in range(3, POOLED):
                        lo_of_pooled(n + m, k + m)
                    if first and c == 0:
                        split_weights(1, range(len(GROUPS)))

            dve.sem_inc(banks_measured, 2)
            nc.vector.memset(x_pad[:, :, :], 0.0).then_inc(pads_zeroed, 1)
            nc.vector.memset(row2[:, :, :], 0.0).then_inc(pads_zeroed, 1)
            nc.vector.memset(row3[:, :, :], 0.0).then_inc(pads_zeroed, 1)
            nc.vector.memset(row3v[:, 0:1, :], 0.0).then_inc(pads_zeroed, 1)
            nc.vector.memset(box[:, :, :], 0.0).then_inc(pads_zeroed, 1)
            nc.vector.memset(ends[:, 0:2, :], 0.0).then_inc(pads_zeroed, 1)
            nc.vector.memset(ends[:, 2 + H:4 + H, :], 0.0).then_inc(pads_zeroed, 1)
            split_weights(0, [0])
            dve.wait_ge(pads_zeroed, 7)
            image_steps(0, 0, first=True)
            image_steps(1, 1)
            with dve.Fori(1, PAIRS) as pair:
                image_steps(2 * pair, 0)
                image_steps(2 * pair + 1, 1)
            measure(IMAGES - 1, 1)

            chain = [0]

            def link(ins):
                chain[0] += 1
                ins.then_inc(bn_chain, 1)
                dve.wait_ge(bn_chain, chain[0])

            dve.wait_ge(banks_measured, IMAGES + 2)
            for o in range(CH):
                link(nc.vector.bn_aggr(moments[:, o, :], stats[:, o].rearrange("p a b -> p (a b)")))
            dve.wait_ge(params_loaded, 48)
            nc.vector.tensor_scalar(var[:, :], moments[:, :, 1], EPS, None, ALU.add).then_inc(var_ready, 1)
            link(add(moments[:, :, 0], moments[:, :, 0], bias[:, :]))
            dve.wait_ge(std_ready, 1)
            link(nc.vector.reciprocal(rstd[:, :], std[:, :]))
            link(nc.vector.tensor_tensor(newton[:, :], rstd[:, :], rstd[:, :], ALU.mult))
            link(nc.vector.tensor_tensor(newton[:, :], newton[:, :], var[:, :], ALU.mult))
            link(nc.vector.tensor_scalar(newton[:, :], newton[:, :], -0.5, 1.5, ALU.mult, ALU.add))
            link(nc.vector.tensor_tensor(rstd[:, :], rstd[:, :], newton[:, :], ALU.mult))
            link(nc.vector.tensor_tensor(bn_scale[:, :], rstd[:, :], gam[:, :], ALU.mult))
            link(nc.vector.tensor_tensor(newton[:, :], moments[:, :, 0], bn_scale[:, :], ALU.mult))
            sub(bn_shift[:, :], bet[:, :], newton[:, :]).then_inc(bn_ready, 1)

            def tail_image_steps(d):
                y_slot, x_slot = slots[d]
                for o in range(CH):
                    nc.vector.scalar_tensor_tensor(
                        out=y_slot[:, o], in0=y_slot[:, o], scalar=bn_scale[:, o:o + 1],
                        in1=x_slot[:, o], op0=ALU.mult, op1=ALU.add).then_inc(scaled, 1)

            tail_image_steps(0)
            for d in range(1, TAIL):
                dve.wait_ge(tail_loaded[d], 32)
                tail_image_steps(d)
            with dve.Fori(1, ROUNDS) as round_:
                dve.wait_ge(tail_loaded[0], 32 * round_)
                tail_image_steps(0)
                for d in range(1, TAIL):
                    dve.wait_ge(tail_loaded[d], 32 * round_ + 32)
                    tail_image_steps(d)

        @block.tensor
        def _(pe):
            def products(parity, c, tap, hi, lo, dy, dx, rows, cols, start, stop):
                for o in range(CH):
                    outs = slice(o * P, (o + 1) * P)
                    for half in range(2):
                        r0 = max(rows[0], half * HALF_ROWS)
                        r1 = min(rows[1], (half + 1) * HALF_ROWS)
                        bank = acc[:, parity, o, half, 0:HALF].rearrange("p (h w) -> p h w", w=W)[
                            :, r0 - half * HALF_ROWS:r1 - half * HALF_ROWS, cols[0]:cols[1]]
                        hi_in, lo_in = (a[:, r0 + dy:r1 + dy, cols[0] + dx:cols[1] + dx] for a in (hi, lo))
                        nc.tensor.matmul(bank, w_hi[c][:, tap, outs], hi_in, start=start, stop=False)
                        nc.tensor.matmul(bank, w_lo[c][:, tap, outs], hi_in, start=False, stop=False)
                        last = nc.tensor.matmul(bank, w_hi[c][:, tap, outs], lo_in, start=False, stop=stop)
                return last

            with pe.Fori(0, PAIRS) as pair:
                for parity in range(2):
                    pe.wait_ge(banks_copied, 2 * pair + parity + 1)
                    pe.wait_ge(banks_measured, 2 * pair + parity + 1)
                    for c in range(CH):
                        s = 4 * pair + 2 * parity + c

                        def weights_split(g):
                            pe.wait_ge(w_lo_ready, c * len(GROUPS) + g + 1)

                        weights_split(0)
                        pe.wait_ge(x_lo_ready, s + 1)
                        for i, (tap, dy, dx) in enumerate(X_TAPS):
                            rows = (max(0, -dy), H - max(0, dy))
                            last = products(parity, c, tap, x_hi[:, c], x_lo[:, c], dy, 1 + dx, rows, (0, W),
                                            start=(c == 0 and i == 0), stop=False)
                        last.then_inc(x_taps_done, 1)
                        weights_split(1)
                        pe.wait_ge(v_lo_ready, s + 1)
                        for tap, dy, dx in V_TAPS:
                            last = products(parity, c, tap, v_hi, v_lo, 1 + dy, 1 + dx, (0, H), (0, W),
                                            start=False, stop=False)
                        last.then_inc(v_taps_done, 1)
                        for m, (rows, cols) in enumerate(PLANES):
                            if m in (0, 2):
                                weights_split(2 + m // 2)
                            slot = (POOLED * c + m) % SPLIT_SLOTS
                            hi, lo = (a[:, slot, 0:plane_size(m)].rearrange("p (h w) -> p h w",
                                                                            w=cols[1] - cols[0])
                                      for a in (pooled_hi, pooled_lo))
                            pe.wait_ge(pooled_lo_ready, POOLED * s + m + 1)
                            products(parity, c, FIRST_POOLED_TAP + m, hi, lo, -rows[0], -cols[0], rows, cols,
                                     start=False, stop=(c == CH - 1 and m == POOLED - 1))\
                                .then_inc(pooled_done, 1)


def kernel(x, L0_conv_w_conv1, L0_conv_w_center, L0_conv_b_center, L0_conv_gamma, L0_conv_beta):
    import numpy as np
    import concourse.bacc as bacc
    from concourse import mybir
    from concourse.bass_utils import run_bass_kernel_spmd

    images, channels, height, width = x.shape
    order = [1, 2, 4, 5, 0, 3, 9, 6, 11, 8, 7, 10]
    w = np.asarray(L0_conv_w_conv1)
    bins = w.shape[2] * w.shape[3]
    w_bins = np.ascontiguousarray(w.reshape(channels, channels, bins).transpose(1, 2, 0)[:, order, :])
    w_center = np.ascontiguousarray(np.asarray(L0_conv_w_center).reshape(channels, channels).transpose(1, 0))

    def per_partition(v):
        return np.ascontiguousarray(np.asarray(v).reshape(-1, 128).T)

    arrays = {
        "x": np.ascontiguousarray(x),
        "w_bins": w_bins,
        "w_center": w_center,
        "b_center": per_partition(L0_conv_b_center),
        "gamma": per_partition(L0_conv_gamma),
        "beta": per_partition(L0_conv_beta),
    }
    nc = bacc.Bacc("TRN2", target_bir_lowering=False, num_devices=1)
    f32 = mybir.dt.float32
    args = [nc.dram_tensor(name, a.shape, f32, kind="ExternalInput").ap() for name, a in arrays.items()]
    out = nc.dram_tensor("out", (images, channels, height, width), f32, kind="ExternalOutput").ap()
    y_dram = nc.dram_tensor("y_dram", (images, 128, channels // 128 * height * width), f32,
                            kind="Internal").ap()
    conv_bn_relu_program(nc, *args, out, y_dram)
    result = run_bass_kernel_spmd(nc, [arrays], core_ids=[0])
    return result.results[0]["out"]
```

```python
from contextlib import ExitStack

import concourse.bass as bass
import numpy as np
from concourse import mybir


def conv_bn_relu_program(nc, x, w_bins, w_center, b_center, gamma, beta, out, y_dram):
    F32 = mybir.dt.float32
    F32R = mybir.dt.float32r
    ALU = mybir.AluOpType
    ACT = mybir.ActivationFunctionType
    AXIS_X = mybir.AxisListType.X

    IMAGES, CHANNELS, H, W = x.shape
    P = 128
    CH = CHANNELS // P
    HW = H * W
    U = W // 2
    HALF = U * H
    EPS = 1e-5
    PAIRS = IMAGES // 2
    CENTER, BELOW, BELOW_LEFT, ABOVE, ABOVE_RIGHT, PAIR_BELOW, PAIR_ABOVE, RIGHT, LEFT, FIRST_POOLED = range(10)
    PLANES = [((0, H), (2, W)),
              ((0, H), (0, W - 2)),
              ((0, H), (0, W - 2)),
              ((0, H), (2, W)),
              ((0, H - 2), (0, W)),
              ((2, H), (0, W))]
    POOLED = len(PLANES)
    PLANE = H * (W - 2)
    TAPS = FIRST_POOLED + POOLED
    GROUPS = [(0, 3, 1.0, 0), (5, 7, 1.0, 0), (3, 5, -1.0, 0),
              (7, 9, 1.0 / 2, 1), (9, 11, 1.0 / 14, 2), (11, 15, 1.0 / 11, 3)]
    GROUP_OF_POOLED = {0: 4, 2: 5}
    LOADS = [(1, 0, 4), (7, 4, 2), (9, 6, 2), (11, 8, 4)]
    SPLIT_SLOTS = 6
    SUM_SLOTS = 4
    TAIL = 13
    PLACES = 2 * (TAIL - 1)
    ROUNDS, REST = divmod(IMAGES, TAIL)

    BANKS = [[0, 2], [4, 0]]
    SHARED = [0, 1]
    COMMON = 6

    x_img = x.rearrange("n (p c) h w -> n p c (h w)", p=P)
    out_img = out.rearrange("n (p c) h w -> n p (c h w)", p=P)
    w_bins_v = w_bins.rearrange("(p c) k o -> p c k o", p=P)
    w_center_v = w_center.rearrange("(p c) o -> p c o", p=P)

    ctx = ExitStack()
    with ctx:
        def sb(name, shape, dt=F32):
            return ctx.enter_context(nc.sbuf_tensor(name, shape, dt))

        def sem(name):
            return ctx.enter_context(nc.semaphore(name))

        start_of, reused_size = {}, [0]
        with ExitStack() as phase1:
            def reused(name, shape, dt=F32):
                start_of[name] = reused_size[0]
                reused_size[0] += -(-int(np.prod(shape[1:])) // 8) * 8
                return phase1.enter_context(nc.sbuf_tensor(name, shape, dt))

            EARLY = 5
            unsplit = reused("unsplit", [P, max(EARLY * CH * HW, CH * TAPS * CHANNELS)])
            w_stage = unsplit[:, 0:CH * TAPS * CHANNELS].rearrange("p (c k o) -> p c k o", c=CH, k=TAPS)
            w_hi = [reused(f"w_hi{c}", [P, TAPS, CHANNELS], F32R) for c in range(CH)]
            w_lo = [reused(f"w_lo{c}", [P, TAPS, CHANNELS], F32R) for c in range(CH)]
            x_split = reused("x_split", [P, CH, 2, W, H + 2], F32R)
            d_split = reused("d_split", [P, 2, W + 1, H + 2], F32R)
            v_split = reused("v_split", [P, 2, W, H + 1], F32R)
            x_hi, x_lo = x_split[:, :, 0], x_split[:, :, 1]
            d_hi, d_lo = d_split[:, 0], d_split[:, 1]
            v_hi, v_lo = v_split[:, 0], v_split[:, 1]
            x_pad = reused("x_pad", [P, W + 4, H + 2])
            row3 = reused("row3", [P, W + 2, H + 3])
            row3v = reused("row3v", [P, W + 2, H + 5])
            box4 = reused("box4", [P, W + 2, H + 3])
            row2 = reused("row2", [P, W + 3, H + 8])
            box3 = reused("box3", [P, W + 2, H + 4])
            ends = reused("ends", [P, W, H + 4])
            pooled = reused("pooled", [P, SUM_SLOTS, PLANE])
            pooled_hi = reused("pooled_hi", [P, SPLIT_SLOTS, PLANE], F32R)
            pooled_lo = reused("pooled_lo", [P, SPLIT_SLOTS, PLANE], F32R)
        phase2 = sb("phase2", [P, reused_size[0]])
        x_stage = sb("x_stage", [P, CH, HW])
        def over_slots(first, rows, cols):
            flat = pooled[:, :, :].rearrange("p a f -> p (a f)")
            return flat[:, first * PLANE:first * PLANE + rows * cols].rearrange("p (w h) -> p w h", h=cols)

        d_sum = [over_slots(2 * c, W + 1, H) for c in range(CH)]
        v_sum = [over_slots(2 - 2 * c, W, H + 1) for c in range(CH)]
        common = sb("common", [P, CH, U, H])
        y_stage = sb("y_stage", [P, CH, HW])
        def place(name, k):
            start = start_of[name] + k * CH * HW
            return phase2[:, start:start + CH * HW].rearrange("p (c f) -> p c f", c=CH)

        assert CH * HW <= FIRST_POOLED * CHANNELS and CH * HW <= min(start_of["x_pad"] - start_of["v_split"],
                                                                     2 * W * (H + 2))
        places = [place("unsplit", k) for k in range(EARLY)]
        places += [place("w_hi0", 0), place("w_lo0", 0), place("x_split", 0)]
        HALF_WINDOWS_END = len(places)
        places += [place("w_hi0", 1), place("w_lo0", 1)]
        HALF_END = len(places)
        assert 2 * CH * HW <= start_of["row2"] - start_of["x_pad"]
        places += [place("x_pad", k) for k in range(2)]
        SUMS_OF_BOX4_END = len(places)
        assert 4 * CH * HW <= start_of["pooled"] - start_of["x_pad"]
        places += [place("x_pad", k) for k in range(2, 4)]
        SUMS_END = len(places)
        places += [place("x_split", 1), place("d_split", 0), place("v_split", 0),
                   place("w_hi1", 0), place("w_lo1", 0)]
        WINDOWS_END = len(places)
        places += [place("x_pad", k) for k in range(4, 6)]
        SPLITS_END = len(places)
        assert CH * HW <= 3 * PLANE and SPLIT_SLOTS == POOLED
        places += [place("pooled_hi", 0), place("pooled_lo", 0)]
        SLOTS_END = len(places)
        places += [place("w_hi1", 1)]
        assert len(places) == PLACES
        slots = [(y_stage, x_stage)] + [(places[k], places[k + 1]) for k in range(0, PLACES, 2)]
        pivot_stats = sb("pivot_stats", [P, CH, 2, 6])
        pivot_moments = sb("pivot_moments", [P, CH, 2])
        minus_pivot = sb("minus_pivot", [P, CH])
        sums = sb("sums", [P, 2, CH, IMAGES])
        totals = sb("totals", [P, 2, CH])
        square = sb("square", [P, CH])
        mean = sb("mean", [P, CH])
        bias = sb("bias", [P, CH])
        gam = sb("gam", [P, CH])
        bet = sb("bet", [P, CH])
        var = sb("var", [P, CH])
        std = sb("std", [P, CH])
        rstd = sb("rstd", [P, CH])
        newton = sb("newton", [P, CH])
        bn_scale = sb("bn_scale", [P, CH])
        bn_shift = sb("bn_shift", [P, CH])
        acc = ctx.enter_context(nc.psum_tensor("acc", [P, 8, 512], F32))

        params_loaded = sem("params_loaded")
        w_loaded = [[sem(f"w_loaded{c}{g}") for g in range(len(LOADS))] for c in range(CH)]
        w_pairs_ready = sem("w_pairs_ready")
        w_hi_ready = sem("w_hi_ready")
        w_lo_ready = sem("w_lo_ready")
        borders_zeroed = sem("borders_zeroed")
        x_loaded = [sem(f"x_loaded{c}") for c in range(CH)]
        x_pad_ready = sem("x_pad_ready")
        x_hi_ready = sem("x_hi_ready")
        x_lo_ready = sem("x_lo_ready")
        warmed_up = sem("warmed_up")
        d_sum_ready = sem("d_sum_ready")
        d_hi_ready = sem("d_hi_ready")
        d_lo_ready = sem("d_lo_ready")
        windows_done = sem("windows_done")
        v_sum_ready = sem("v_sum_ready")
        v_hi_ready = sem("v_hi_ready")
        v_lo_ready = sem("v_lo_ready")
        row2_ready = sem("row2_ready")
        row3_ready = sem("row3_ready")
        row3v_ready = sem("row3v_ready")
        box3_ready = sem("box3_ready")
        box4_ready = sem("box4_ready")
        ends_ready = sem("ends_ready")
        pooled_ready = sem("pooled_ready")
        pooled_hi_ready = sem("pooled_hi_ready")
        pooled_lo_ready = sem("pooled_lo_ready")
        pooled_done = sem("pooled_done")
        common_copied = sem("common_copied")
        banks_taken = sem("banks_taken")
        pivot_ready = sem("pivot_ready")
        y_measured = sem("y_measured")
        y_saved = sem("y_saved")
        bn_chain = sem("bn_chain")
        var_ready = sem("var_ready")
        std_ready = sem("std_ready")
        bn_ready = sem("bn_ready")
        tail_loaded = [sem(f"tail_loaded{d}") for d in range(TAIL)]
        scaled = sem("scaled")
        relu_done = sem("relu_done")
        stored = [sem(f"stored{d}") for d in range(TAIL)]

        BORDERS = 19
        WARM_UP = 20
        KINDS = 2
        MOMENTS = KINDS * CH
        BANKS_FREE = 3
        COMMON_FREE = 1

        def wait_from_one(engine, semaphore, count):
            if isinstance(count, int) and count <= 0:
                return
            engine.wait_ge(semaphore, count)

        def plane_size(m):
            (h0, h1), (w0, w1) = PLANES[m]
            return (h1 - h0) * (w1 - w0)

        def tail_image(round_, d):
            return TAIL * round_ + d - 1

        block = ctx.enter_context(nc.Block())

        @block.gpsimd
        def _(pool):
            n = 0
            for edge in (std[:, :], pooled_hi[:, 0, 0:HALF],
                         x_pad[:, 0:2, :], x_pad[:, W + 2:W + 4, :], x_pad[:, 2:W + 2, 0:H + 2:H + 1],
                         x_hi[:, 0, :, 0:H + 2:H + 1], x_lo[:, 0, :, 0:H + 2:H + 1],
                         x_hi[:, 1, :, 0:H + 2:H + 1], x_lo[:, 1, :, 0:H + 2:H + 1],
                         d_hi[:, :, 0:H + 2:H + 1], d_lo[:, :, 0:H + 2:H + 1],
                         row2[:, :, :],
                         row3[:, :, 0:1], row3[:, :, H + 1:H + 3],
                         row3v[:, :, 0:2], row3v[:, :, H + 3:H + 5],
                         box3[:, :, 0:H + 4:H + 3],
                         ends[:, :, 0:2], ends[:, :, H + 2:H + 4]):
                if edge.dtype == F32R:
                    edge = edge.bitcast(F32)
                nc.gpsimd.memset(edge, 0.0).then_inc(borders_zeroed, 1)
                n += 1
            assert n == BORDERS

        @block.sync
        def _(sp):
            def load_set(image, c):
                sp.dma_start(x_stage[:, c],
                             x_img[bass.ds(image, 1), :, c].rearrange("n p f -> p (n f)"))\
                    .then_inc(x_loaded[c], 16)

            def load_weights(c):
                sp.dma_start(w_stage[:, c, CENTER, :], w_center_v[:, c, :]).then_inc(w_loaded[c][0], 16)
                for g, (tap, first, count) in enumerate(LOADS):
                    sp.dma_start(w_stage[:, c, tap:tap + count, :], w_bins_v[:, c, first:first + count, :])\
                        .then_inc(w_loaded[c][g], 16)

            def image_steps(image, first=False, last=False):
                if not last:
                    for c in range(CH):
                        sp.wait_ge(x_lo_ready, 2 * image + c + 1)
                        load_set(image + 1, c)
                if not first:
                    sp.wait_ge(banks_taken, 2 * image + BANKS_FREE)
                    sp.dma_start(y_dram[bass.ds(image - 1, 1)].rearrange("n p f -> p (n f)"),
                                 y_stage[:, :, :].rearrange("p c f -> p (c f)")).then_inc(y_saved, 16)

            def load_y(round_, d):
                sp.dma_start(slots[d][0][:, :, :].rearrange("p c f -> p (c f)"),
                             y_dram[bass.ds(tail_image(round_, d), 1)].rearrange("n p f -> p (n f)"))\
                    .then_inc(tail_loaded[d], 16)

            def load_x(round_, d):
                sp.dma_start(slots[d][1][:, :, :].rearrange("p c f -> p (c f)"),
                             x_img[bass.ds(tail_image(round_, d), 1)].rearrange("n p c f -> p (n c f)"))\
                    .then_inc(tail_loaded[d], 16)

            def load_places(first, end):
                for k in range(first, end):
                    (load_x if k % 2 else load_y)(0, 1 + k // 2)

            def reload(round_, d):
                sp.wait_ge(stored[d], 16 * round_)
                load_y(round_, d)
                load_x(round_, d)

            load_set(0, 0)
            load_weights(0)
            load_set(0, 1)
            load_weights(1)
            for dst, src in ((bias, b_center), (gam, gamma), (bet, beta)):
                sp.dma_start(dst[:, :], src).then_inc(params_loaded, 16)
            image_steps(0, first=True)
            with sp.Fori(1, IMAGES - 1) as image:
                image_steps(image)
            sp.wait_ge(y_saved, 16 * TAIL)
            sp.wait_ge(w_lo_ready, CH * len(GROUPS))
            load_places(0, EARLY)
            image_steps(IMAGES - 1, last=True)
            sp.wait_ge(windows_done, 2 * IMAGES - 1)
            load_places(EARLY, HALF_WINDOWS_END)
            sp.wait_ge(pooled_done, POOLED * (2 * IMAGES - 1))
            load_places(HALF_WINDOWS_END, HALF_END)
            sp.wait_ge(pooled_ready, POOLED * (2 * IMAGES - 1) + 2)
            load_places(HALF_END, SUMS_OF_BOX4_END)
            sp.wait_ge(pooled_ready, POOLED * 2 * IMAGES)
            load_places(SUMS_OF_BOX4_END, SUMS_END)
            sp.wait_ge(windows_done, 2 * IMAGES)
            load_places(SUMS_END, WINDOWS_END)
            sp.wait_ge(pooled_lo_ready, POOLED * 2 * IMAGES)
            load_places(WINDOWS_END, SPLITS_END)
            sp.wait_ge(pooled_done, POOLED * (2 * IMAGES - 1) + 3)
            load_places(SPLITS_END, SLOTS_END)
            sp.wait_ge(pooled_done, POOLED * 2 * IMAGES)
            load_places(SLOTS_END, PLACES)
            sp.wait_ge(y_saved, 16 * (IMAGES - 1))
            with sp.Fori(1, ROUNDS) as round_:
                for d in range(TAIL):
                    reload(round_, d)
            for d in range(REST):
                reload(ROUNDS, d)
            for d in range(TAIL):
                sp.wait_ge(stored[d], 16 * (ROUNDS + (d < REST)))

        @block.scalar
        def _(act):
            def split_weights(c, groups):
                for g in groups:
                    a, b, factor, load = GROUPS[g]
                    act.wait_ge(w_loaded[c][load], 32 if load == 0 else 16)
                    if a == PAIR_BELOW:
                        act.wait_ge(w_pairs_ready, c + 1)
                    nc.scalar.activation(w_hi[c][:, a:b, :], w_stage[:, c, a:b, :], ACT.Copy,
                                         scale=factor).then_inc(w_hi_ready, 1)

            def spread_x(s, c, image):
                act.wait_ge(x_loaded[c], 16 * (image + 1))
                x_in = x_stage[:, c].rearrange("p (h w) -> p w h", w=W)
                nc.scalar.activation(x_pad[:, 2:W + 2, 1:H + 1], x_in, ACT.Copy).then_inc(x_pad_ready, 1)
                wait_from_one(act, windows_done, s - 1)
                nc.scalar.activation(x_hi[:, c, :, 1:H + 1], x_in, ACT.Copy).then_inc(x_hi_ready, 1)

            def split_pooled(n, k):
                size = plane_size(k % POOLED)
                wait_from_one(act, pooled_done, n - SPLIT_SLOTS + 1)
                act.wait_ge(pooled_ready, n + 1)
                nc.scalar.activation(pooled_hi[:, k % SPLIT_SLOTS, 0:size], pooled[:, k % SUM_SLOTS, 0:size],
                                     ACT.Copy).then_inc(pooled_hi_ready, 1)

            def measure(image, o):
                act.wait_ge(banks_taken, 2 * (image + 1) + BANKS_FREE)
                act.wait_ge(pivot_ready, 1)
                act.wait_ge(common_copied, image + 1 + COMMON_FREE)
                used_up = common[:, :, :, :].rearrange("p c u h -> p (c u h)")
                for kind, function in enumerate((ACT.Identity, ACT.Square)):
                    wait_from_one(act, y_measured, MOMENTS * image + KINDS * o + kind)
                    nc.scalar.activation(used_up, y_stage[:, o], function, bias=minus_pivot[:, o:o + 1],
                                         accum_out=sums[:, kind, o, bass.ds(image, 1)]).then_inc(y_measured, 1)

            def image_steps(image, first=False, last=False):
                for c in range(CH):
                    s = 2 * image + c
                    n = POOLED * s
                    k = POOLED * c
                    wait_from_one(act, windows_done, s)
                    act.wait_ge(d_sum_ready, s + 1)
                    nc.scalar.activation(d_hi[:, :, 1:H + 1], d_sum[c], ACT.Copy).then_inc(d_hi_ready, 1)
                    act.wait_ge(v_sum_ready, s + 1)
                    nc.scalar.activation(v_hi[:, :, :], v_sum[c], ACT.Copy).then_inc(v_hi_ready, 1)
                    if c == 1 and not first:
                        measure(image - 1, 1)
                    if first and c == 0:
                        split_weights(0, [3, 4, 5])
                        split_weights(1, [0])
                        act.wait_ge(warmed_up, 1)
                    split_pooled(n, k)
                    split_pooled(n + 1, k + 1)
                    if first and c == 0:
                        split_weights(1, [1, 2, 3])
                    if not (last and c == CH - 1):
                        spread_x(s + 1, 1 - c, image + c)
                    for m in range(2, POOLED - 1):
                        split_pooled(n + m, k + m)
                    if c == CH - 1:
                        act.wait_ge(windows_done, s + 1)
                        wait_from_one(act, y_measured, MOMENTS * image)
                        nc.scalar.activation(common[:, :, :, :].rearrange("p c u h -> p c (u h)"),
                                             acc[:, COMMON:COMMON + CH, 0:HALF], ACT.Copy)\
                            .then_inc(common_copied, 1)
                    if first and c == 0:
                        split_weights(1, [4, 5])
                    split_pooled(n + POOLED - 1, k + POOLED - 1)
                    if c == 0 and not first:
                        measure(image - 1, 0)

            def store(round_, d):
                image = IMAGES - 1 if isinstance(round_, int) and round_ == d == 0 else tail_image(round_, d)
                act.dma_start(out_img[bass.ds(image, 1)].rearrange("n p f -> p (n f)"),
                              slots[d][1][:, :, :].rearrange("p c f -> p (c f)")).then_inc(stored[d], 16)

            def tail_round(round_, count):
                for d in range(count):
                    turn = round_ * TAIL + d
                    x_slot = slots[d][1]
                    for o in range(CH):
                        act.wait_ge(scaled, CH * turn + o + 1)
                        nc.scalar.activation(x_slot[:, o], x_slot[:, o], ACT.Relu,
                                             bias=bn_shift[:, o:o + 1]).then_inc(relu_done, 1)
                    act.wait_ge(relu_done, CH * (turn + 1))
                    store(round_, d)

            act.sem_inc(common_copied, COMMON_FREE)
            act.wait_ge(borders_zeroed, 1)
            nc.scalar.activation(std[:, :], std[:, :], ACT.Sqrt)
            act.wait_ge(borders_zeroed, BORDERS)
            spread_x(0, 0, 0)
            split_weights(0, [0, 1, 2])
            image_steps(0, first=True)
            with act.Fori(1, IMAGES - 1) as image:
                image_steps(image)
            image_steps(IMAGES - 1, last=True)
            for o in range(CH):
                measure(IMAGES - 1, o)

            act.wait_ge(var_ready, 1)
            nc.scalar.activation(std[:, :], var[:, :], ACT.Sqrt).then_inc(std_ready, 1)
            act.wait_ge(bn_ready, 1)
            tail_round(0, TAIL)
            with act.Fori(1, ROUNDS) as round_:
                tail_round(round_, TAIL)
            tail_round(ROUNDS, REST)

        @block.vector
        def _(dve):
            add = lambda out_, a, b: nc.vector.tensor_tensor(out_, a, b, ALU.add)
            sub = lambda out_, a, b: nc.vector.tensor_tensor(out_, a, b, ALU.subtract)
            chain = [0]

            def link(ins):
                chain[0] += 1
                ins.then_inc(bn_chain, 1)
                dve.wait_ge(bn_chain, chain[0])

            def pair_weights(c):
                dve.wait_ge(w_loaded[c][0], 32)
                add(w_stage[:, c, PAIR_BELOW:PAIR_ABOVE + 1, :], w_stage[:, c, BELOW:ABOVE_RIGHT + 1:2, :],
                    w_stage[:, c, BELOW + 1:ABOVE_RIGHT + 1:2, :]).then_inc(w_pairs_ready, 1)

            def lo_of_weights(c, groups):
                for g in groups:
                    a, b, factor, _ = GROUPS[g]
                    dve.wait_ge(w_hi_ready, c * len(GROUPS) + g + 1)
                    nc.vector.scalar_tensor_tensor(
                        out=w_lo[c][:, a:b, :].rearrange("p k o -> p (k o)"),
                        in0=w_stage[:, c, a:b, :].rearrange("p k o -> p (k o)"), scalar=factor,
                        in1=w_hi[c][:, a:b, :].bitcast(F32).rearrange("p k o -> p (k o)"),
                        op0=ALU.mult, op1=ALU.subtract).then_inc(w_lo_ready, 1)

            def piece(source, left, top, m, dw, dh):
                (h0, h1), (w0, w1) = PLANES[m]
                return source[:, w0 + dw - left:w1 + dw - left, h0 + dh - top:h1 + dh - top]

            def box3_at(m, dw, dh):
                return piece(box3, -1, -2, m, dw, dh)

            def box4_at(m, dw, dh):
                return piece(box4, -1, -3, m, dw, dh)

            def row2_at(m, dw, dh):
                return piece(row2, -2, -4, m, dw, dh)

            def ends_at(m, dh):
                return piece(ends, 0, -2, m, 0, dh)

            def lo_of_pooled(n, k):
                size = plane_size(k % POOLED)
                dve.wait_ge(pooled_hi_ready, n + 1)
                sub(pooled_lo[:, k % SPLIT_SLOTS, 0:size], pooled[:, k % SUM_SLOTS, 0:size],
                    pooled_hi[:, k % SPLIT_SLOTS, 0:size].bitcast(F32)).then_inc(pooled_lo_ready, 1)

            def take_banks(image, parity):
                dve.wait_ge(pooled_done, 2 * POOLED * (image + 1))
                dve.wait_ge(common_copied, image + 1 + COMMON_FREE)
                wait_from_one(dve, y_saved, 16 * image)
                wait_from_one(dve, y_measured, MOMENTS * image)
                for o in (SHARED[parity], 1 - SHARED[parity]):
                    bank = BANKS[parity][o]
                    y_out = y_stage[:, o].rearrange("p (u q h) -> p q u h", q=2, h=H)
                    terms = common[:, o].rearrange("p (q u) h -> p q u h", q=1).to_broadcast([P, 2, U, H])
                    add(y_out, acc[:, bank:bank + 2, 0:HALF].rearrange("p q (u h) -> p q u h", h=H),
                        terms).then_inc(banks_taken, 1)

            def make_pivot():
                dve.wait_ge(banks_taken, 2 + BANKS_FREE)
                for o in range(CH):
                    for half in range(2):
                        link(nc.vector.bn_stats(pivot_stats[:, o, half, :],
                                                y_stage[:, o, half * HALF:(half + 1) * HALF]))
                for o in range(CH):
                    link(nc.vector.bn_aggr(pivot_moments[:, o, :],
                                           pivot_stats[:, o].rearrange("p a b -> p (a b)")))
                nc.vector.tensor_scalar(minus_pivot[:, :], pivot_moments[:, :, 0], -1.0, None, ALU.mult)\
                    .then_inc(pivot_ready, 1)

            def image_steps(image, parity, first=False, second=False):
                for c in range(CH):
                    s = 2 * image + c
                    n = POOLED * s
                    k = POOLED * c

                    def pooled_sum(m, a, b):
                        wait_from_one(dve, pooled_lo_ready, n + m - SUM_SLOTS + 1)
                        if m == 0:
                            dve.wait_ge(d_lo_ready, s + 1)
                        if m == 2:
                            dve.wait_ge(v_lo_ready, s + 1)
                        (_, _), (w0, w1) = PLANES[m]
                        slot = pooled[:, (k + m) % SUM_SLOTS, 0:plane_size(m)]
                        add(slot.rearrange("p (w h) -> p w h", w=w1 - w0), a, b).then_inc(pooled_ready, 1)

                    dve.wait_ge(x_hi_ready, s + 1)
                    sub(x_lo[:, c, :, 1:H + 1], x_stage[:, c].rearrange("p (h w) -> p w h", w=W),
                        x_hi[:, c, :, 1:H + 1].bitcast(F32)).then_inc(x_lo_ready, 1)
                    if first:
                        lo_of_weights(c, [0])
                        if c == 0:
                            pair_weights(0)
                    dve.wait_ge(x_pad_ready, s + 1)
                    wait_from_one(dve, pooled_lo_ready, n - 2)
                    sub(d_sum[c][:, 0:W + 1:2, :], x_pad[:, 1:2 + W:2, 1:1 + H], x_pad[:, 2:3 + W:2, 1:1 + H])
                    sub(d_sum[c][:, 1:W:2, :], x_pad[:, 3:3 + W:2, 1:1 + H], x_pad[:, 2:2 + W:2, 1:1 + H])\
                        .then_inc(d_sum_ready, 1)
                    if first:
                        lo_of_weights(c, [1])
                    wait_from_one(dve, pooled_lo_ready, n)
                    add(v_sum[c], x_pad[:, 2:2 + W, 0:H + 1], x_pad[:, 2:2 + W, 1:H + 2])\
                        .then_inc(v_sum_ready, 1)
                    if first:
                        lo_of_weights(c, [2])
                    dve.wait_ge(d_hi_ready, s + 1)
                    sub(d_lo[:, :, 1:H + 1], d_sum[c], d_hi[:, :, 1:H + 1].bitcast(F32))\
                        .then_inc(d_lo_ready, 1)
                    wait_from_one(dve, pooled_ready, n)
                    add(row2[:, 1:2 + W, 4:4 + H], x_pad[:, 1:2 + W, 1:1 + H],
                        x_pad[:, 2:3 + W, 1:1 + H]).then_inc(row2_ready, 1)
                    dve.wait_ge(v_hi_ready, s + 1)
                    sub(v_lo[:, :, :], v_sum[c], v_hi[:, :, :].bitcast(F32)).then_inc(v_lo_ready, 1)
                    if first:
                        lo_of_weights(c, [3])
                    dve.wait_ge(row2_ready, s + 1)
                    add(row3[:, :, 1:1 + H], row2[:, 0:2 + W, 4:4 + H], x_pad[:, 2:4 + W, 1:1 + H])\
                        .then_inc(row3_ready, 1)
                    add(ends[:, :, 2:2 + H], x_pad[:, 0:W, 1:1 + H], x_pad[:, 4:4 + W, 1:1 + H])\
                        .then_inc(ends_ready, 1)
                    dve.wait_ge(row3_ready, s + 1)
                    add(row3v[:, :, 2:3 + H], row3[:, :, 0:1 + H], row3[:, :, 1:2 + H])\
                        .then_inc(row3v_ready, 1)
                    if first and c == 0:
                        pair_weights(1)
                    if c == 0 and not first:
                        take_banks(image - 1, 1 - parity)
                    dve.wait_ge(row3v_ready, s + 1)
                    add(box4[:, :, :], row3v[:, :, 0:3 + H], row3v[:, :, 2:5 + H]).then_inc(box4_ready, 1)
                    add(box3[:, :, 1:3 + H], row3v[:, :, 1:3 + H], row3[:, :, 1:3 + H])\
                        .then_inc(box3_ready, 1)
                    dve.wait_ge(box4_ready, s + 1)
                    pooled_sum(0, box4_at(0, -3, -3), row2_at(0, -4, -4))
                    pooled_sum(1, box4_at(1, 3, 0), row2_at(1, 3, 4))
                    if first:
                        lo_of_weights(c, [4])
                        lo_of_pooled(n, k)
                    dve.wait_ge(box3_ready, s + 1)
                    pooled_sum(2, box3_at(2, 3, -2), row2_at(2, 3, -4))
                    if first:
                        lo_of_weights(c, [5])
                    else:
                        lo_of_pooled(n, k)
                    pooled_sum(3, box3_at(3, -3, 2), row2_at(3, -4, 4))
                    lo_of_pooled(n + 1, k + 1)
                    dve.wait_ge(ends_ready, s + 1)
                    pooled_sum(4, box3_at(4, 0, 3), ends_at(4, 4))
                    lo_of_pooled(n + 2, k + 2)
                    pooled_sum(5, box3_at(5, 0, -3), ends_at(5, -4))
                    for m in range(3, POOLED):
                        lo_of_pooled(n + m, k + m)
                    if second and c == 0:
                        make_pivot()

            dve.sem_inc(banks_taken, BANKS_FREE)
            dve.wait_ge(borders_zeroed, BORDERS)
            image_steps(0, 0, first=True)
            image_steps(1, 1, second=True)
            with dve.Fori(1, PAIRS) as pair:
                image_steps(2 * pair, 0)
                image_steps(2 * pair + 1, 1)
            take_banks(IMAGES - 1, 1)

            dve.wait_ge(y_measured, MOMENTS * IMAGES)
            link(nc.vector.reduce_sum(totals[:, :, :], sums[:, :, :, :], AXIS_X))
            link(nc.vector.tensor_scalar(totals[:, :, :], totals[:, :, :], 1.0 / (IMAGES * HW), None, ALU.mult))
            link(nc.vector.tensor_tensor(square[:, :], totals[:, 0, :], totals[:, 0, :], ALU.mult))
            link(sub(var[:, :], totals[:, 1, :], square[:, :]))
            nc.vector.tensor_scalar(var[:, :], var[:, :], 0.0, EPS, ALU.max, ALU.add).then_inc(var_ready, 1)
            dve.wait_ge(params_loaded, 48)
            dve.wait_ge(pivot_ready, 1)
            link(sub(mean[:, :], totals[:, 0, :], minus_pivot[:, :]))
            link(add(mean[:, :], mean[:, :], bias[:, :]))
            link(sub(bn_shift[:, :], bias[:, :], mean[:, :]))
            dve.wait_ge(std_ready, 1)
            link(nc.vector.reciprocal(rstd[:, :], std[:, :]))
            link(nc.vector.tensor_tensor(newton[:, :], rstd[:, :], rstd[:, :], ALU.mult))
            link(nc.vector.tensor_tensor(newton[:, :], newton[:, :], var[:, :], ALU.mult))
            link(nc.vector.tensor_scalar(newton[:, :], newton[:, :], -0.5, 1.5, ALU.mult, ALU.add))
            link(nc.vector.tensor_tensor(rstd[:, :], rstd[:, :], newton[:, :], ALU.mult))
            link(nc.vector.tensor_tensor(bn_scale[:, :], rstd[:, :], gam[:, :], ALU.mult))
            link(nc.vector.tensor_tensor(bn_shift[:, :], bn_shift[:, :], bn_scale[:, :], ALU.mult))
            add(bn_shift[:, :], bn_shift[:, :], bet[:, :]).then_inc(bn_ready, 1)

            def scale_image(d):
                y_slot, x_slot = slots[d]
                for o in range(CH):
                    x_t = x_slot[:, o].rearrange("p (h w) -> p w h", w=W)
                    nc.vector.scalar_tensor_tensor(
                        out=x_t, in0=y_slot[:, o].rearrange("p (w h) -> p w h", h=H),
                        scalar=bn_scale[:, o:o + 1], in1=x_t, op0=ALU.mult, op1=ALU.add).then_inc(scaled, 1)

            def scale_loaded(round_, d):
                dve.wait_ge(tail_loaded[d], 32 * round_ if d == 0 else 32 * round_ + 32)
                scale_image(d)

            scale_image(0)
            for d in range(1, TAIL):
                scale_loaded(0, d)
            with dve.Fori(1, ROUNDS) as round_:
                for d in range(TAIL):
                    scale_loaded(round_, d)
            for d in range(REST):
                scale_loaded(ROUNDS, d)

        @block.tensor
        def _(pe):
            def products(c, o, tap, bank, hi, lo, us, hs, w0, h0, start=False, stop=False):
                outs = slice(o * P, (o + 1) * P)
                place = acc[:, bank, 0:HALF].rearrange("p (u h) -> p u h", h=H)[:, us[0]:us[1], hs[0]:hs[1]]
                hi_in, lo_in = (a[:, w0:w0 + 2 * (us[1] - us[0]) - 1:2, h0:h0 + hs[1] - hs[0]]
                                for a in (hi, lo))
                nc.tensor.matmul(place, w_hi[c][:, tap, outs], hi_in, start=start, stop=False)
                nc.tensor.matmul(place, w_lo[c][:, tap, outs], hi_in, start=False, stop=False)
                return nc.tensor.matmul(place, w_hi[c][:, tap, outs], lo_in, start=False, stop=stop)

            ALL_U, ALL_H = (0, U), (0, H)

            pe.wait_ge(borders_zeroed, 2)
            zeros = pooled_hi[:, 0, 0:HALF]
            for k in range(WARM_UP):
                warm = nc.tensor.matmul(acc[:, BANKS[0][1], 0:HALF], zeros[:, 0:P], zeros,
                                        start=True, stop=True)
            warm.then_inc(warmed_up, 1)

            with pe.Fori(0, PAIRS) as pair:
                for parity in range(2):
                    image = 2 * pair + parity
                    for c in range(CH):
                        s = 2 * image + c
                        start = c == 0

                        def weights_split(g):
                            pe.wait_ge(w_lo_ready, c * len(GROUPS) + g + 1)

                        weights_split(0)
                        pe.wait_ge(x_lo_ready, s + 1)
                        xs = (x_hi[:, c], x_lo[:, c])
                        if c == 0:
                            pe.wait_ge(banks_taken, 2 * image - 2 + BANKS_FREE)
                            pe.wait_ge(common_copied, image + COMMON_FREE)
                        for o in (1 - SHARED[parity], SHARED[parity]):
                            even = BANKS[parity][o]
                            odd = even + 1
                            shared = o == SHARED[parity]
                            if c == 0 and shared:
                                pe.wait_ge(banks_taken, 2 * image - 1 + BANKS_FREE)
                            products(c, o, CENTER, even, *xs, ALL_U, ALL_H, 0, 1, start=start)
                            products(c, o, CENTER, odd, *xs, ALL_U, ALL_H, 1, 1, start=start)
                            if not shared:
                                weights_split(1)
                            products(c, o, PAIR_BELOW, COMMON + o, *xs, ALL_U, ALL_H, 0, 2, start=start)
                            products(c, o, PAIR_ABOVE, COMMON + o, *xs, ALL_U, ALL_H, 1, 0, stop=not start)
                            if not shared:
                                weights_split(2)
                                pe.wait_ge(d_lo_ready, s + 1)
                            products(c, o, BELOW_LEFT, even, d_hi, d_lo, ALL_U, ALL_H, 0, 2)
                            products(c, o, BELOW, odd, d_hi, d_lo, ALL_U, ALL_H, 1, 2)
                            products(c, o, ABOVE, even, d_hi, d_lo, ALL_U, ALL_H, 1, 0)
                            products(c, o, ABOVE_RIGHT, odd, d_hi, d_lo, ALL_U, ALL_H, 2, 0)
                            if not shared:
                                weights_split(3)
                                pe.wait_ge(v_lo_ready, s + 1)
                            products(c, o, RIGHT, even, v_hi, v_lo, ALL_U, ALL_H, 1, 1)
                            products(c, o, RIGHT, odd, v_hi, v_lo, (0, U - 1), ALL_H, 2, 1)
                            products(c, o, LEFT, even, v_hi, v_lo, (1, U), ALL_H, 1, 0)
                            last = products(c, o, LEFT, odd, v_hi, v_lo, ALL_U, ALL_H, 0, 0)
                        last.then_inc(windows_done, 1)
                        for m, (hs, (w0, w1)) in enumerate(PLANES):
                            if m in GROUP_OF_POOLED:
                                weights_split(GROUP_OF_POOLED[m])
                            slot = (POOLED * c + m) % SPLIT_SLOTS
                            hi, lo = (a[:, slot, 0:plane_size(m)].rearrange("p (w h) -> p w h", w=w1 - w0)
                                      for a in (pooled_hi, pooled_lo))
                            us = (w0 // 2, w1 // 2)
                            pe.wait_ge(pooled_lo_ready, POOLED * s + m + 1)
                            for o in range(CH):
                                for q in range(2):
                                    last = products(c, o, FIRST_POOLED + m, BANKS[parity][o] + q, hi, lo,
                                                    us, hs, q, 0, stop=(c == CH - 1 and m == POOLED - 1))
                            last.then_inc(pooled_done, 1)


def kernel(x, L0_conv_w_conv1, L0_conv_w_center, L0_conv_b_center, L0_conv_gamma, L0_conv_beta):
    import numpy as np
    import concourse.bacc as bacc
    from concourse import mybir
    from concourse.bass_utils import run_bass_kernel_spmd

    images, channels, height, width = x.shape
    order = [1, 2, 4, 5, 0, 3, 9, 6, 11, 8, 7, 10]
    w = np.asarray(L0_conv_w_conv1)
    bins = w.shape[2] * w.shape[3]
    halves = np.arange(channels).reshape(128, -1).T.reshape(-1)
    w_bins = np.ascontiguousarray(
        w.reshape(channels, channels, bins).transpose(1, 2, 0)[:, order][:, :, halves])
    w_center = np.ascontiguousarray(
        np.asarray(L0_conv_w_center).reshape(channels, channels).transpose(1, 0)[:, halves])

    def per_partition(v):
        return np.ascontiguousarray(np.asarray(v).reshape(128, -1))

    arrays = {
        "x": np.ascontiguousarray(x),
        "w_bins": w_bins,
        "w_center": w_center,
        "b_center": per_partition(L0_conv_b_center),
        "gamma": per_partition(L0_conv_gamma),
        "beta": per_partition(L0_conv_beta),
    }
    nc = bacc.Bacc("TRN2", target_bir_lowering=False, num_devices=1)
    f32 = mybir.dt.float32
    args = [nc.dram_tensor(name, a.shape, f32, kind="ExternalInput").ap() for name, a in arrays.items()]
    out = nc.dram_tensor("out", (images, channels, height, width), f32, kind="ExternalOutput").ap()
    y_dram = nc.dram_tensor("y_dram", (images, 128, channels // 128 * height * width), f32,
                            kind="Internal").ap()
    conv_bn_relu_program(nc, *args, out, y_dram)
    result = run_bass_kernel_spmd(nc, [arrays], core_ids=[0])
    return result.results[0]["out"]
```
